# Optimizing a Trainium2 kernel written in Bass

```python
import numpy as np
import jax
import jax.numpy as jnp

def _softmax(x, axis=-1):
    return jax.nn.softmax(x, axis=axis)

def _gelu(x):
    return jax.nn.gelu(x, approximate=True)

def _silu(x):
    return jax.nn.silu(x)

def _sigmoid(x):
    return jax.nn.sigmoid(x)

def _layernorm(x, axis=-1, eps=1e-05):
    m = jnp.mean(x, axis=axis, keepdims=True)
    v = jnp.var(x, axis=axis, keepdims=True)
    return (x - m) / jnp.sqrt(v + eps)

def _scatter_add(tgt, idx, src, axis=0):
    return tgt.at[idx].add(src)

def _segment_sum(src, seg, n):
    return jax.ops.segment_sum(src, seg, n)
kernel_name = 'mk_pixart_seq_d1_seqx_r2_338e10'

def setup_inputs(seed: int=0):
    np.random.seed(seed)
    _w = jnp.asarray

    def _rec_inputs():
        import jax
        import jax.numpy as jnp
        _rk = jax.random.key(seed)
        x = -0.0003929 + 0.9999 * jax.random.normal(jax.random.fold_in(_rk, 1), (1, 4096, 512), jnp.float32)
        _lenS = 4096 - jax.random.randint(jax.random.fold_in(_rk, 7), (1,), 0, max(1, 4096 // 4) + 1, jnp.int32)
        _lenS2 = 3202 - jax.random.randint(jax.random.fold_in(_rk, 8), (1,), 0, max(1, 3202 // 4) + 1, jnp.int32)
        _ctx_1024P = jax.random.normal(jax.random.fold_in(_rk, 11), (1, 16, 512), jnp.float32)
        _ctx_1024c = jax.random.dirichlet(jax.random.fold_in(_rk, 511), 0.3 * jnp.ones((16,), jnp.float32), (1, 3202))
        _ctx_1024t = jnp.einsum('bsk,bkd->bsd', _ctx_1024c, _ctx_1024P)
        _ctx_1024t = _ctx_1024t * jax.lax.rsqrt(jnp.mean(jnp.square(_ctx_1024t)) + 1e-12) * 0.953939
        ctx_1024 = -1.39393e-06 + 0.999914 * (_ctx_1024t + 0.3 * jax.random.normal(jax.random.fold_in(_rk, 611), (1, 3202, 512), jnp.float32))
        cond_1024 = -0.00920427 + 1.00102 * jax.random.normal(jax.random.fold_in(_rk, 12), (1, 512), jnp.float32)
        return (x, ctx_1024, cond_1024)
    x, ctx_1024, cond_1024 = _rec_inputs()

    def _L0_xcond_setup():
        import jax, jax.numpy as jnp
        import numpy as np
        EPS = 1e-05

        def _ada_ln(x, c, W_ss, b_ss):
            mu = jnp.mean(x, axis=-1, keepdims=True)
            var = jnp.mean((x - mu) ** 2, axis=-1, keepdims=True)
            h = (x - mu) / jnp.sqrt(var + EPS)
            ss = jax.nn.silu(c) @ W_ss + b_ss
            scale, bias = jnp.split(ss, 2, axis=-1)
            return (1.0 + scale)[:, None, :] * h + bias[:, None, :]
        key = jax.random.key(seed)
        ks = jax.random.split(key, 12)
        B, Lq, Lkv, H = (8, 1024, 256, 512)
        s = 0.02
        return {'x_q': jax.random.normal(ks[0], (B, Lq, H), jnp.float32), 'x_kv': jax.random.normal(ks[1], (B, Lkv, H), jnp.float32), 't_vec': jax.random.normal(ks[2], (B, H), jnp.float32), 'Wq': jax.random.normal(ks[3], (H, H), jnp.float32) * s, 'bq': jnp.zeros((H,), jnp.float32), 'Wkv': jax.random.normal(ks[4], (H, 2 * H), jnp.float32) * s, 'bkv': jnp.zeros((2 * H,), jnp.float32), 'Wp': jax.random.normal(ks[5], (H, H), jnp.float32) * s, 'bp': jnp.zeros((H,), jnp.float32), 'Wss_q': jax.random.normal(ks[6], (H, 2 * H), jnp.float32) * s, 'bss_q': jnp.zeros((2 * H,), jnp.float32), 'Wss_kv': jax.random.normal(ks[7], (H, 2 * H), jnp.float32) * s, 'bss_kv': jnp.zeros((2 * H,), jnp.float32)}
    _L0_xcond_all = _L0_xcond_setup()
    _L0_xcond_in = {k: v for k, v in _L0_xcond_all.items() if k in ('Wq', 'bq', 'Wkv', 'bkv', 'Wp', 'bp', 'Wss_q', 'bss_q', 'Wss_kv', 'bss_kv')}
    del _L0_xcond_all
    return {'x': x, 'ctx_1024': ctx_1024, 'cond_1024': cond_1024, 'L0_xcond_Wq': _L0_xcond_in['Wq'], 'L0_xcond_bq': _L0_xcond_in['bq'], 'L0_xcond_Wkv': _L0_xcond_in['Wkv'], 'L0_xcond_bkv': _L0_xcond_in['bkv'], 'L0_xcond_Wp': _L0_xcond_in['Wp'], 'L0_xcond_bp': _L0_xcond_in['bp'], 'L0_xcond_Wss_q': _L0_xcond_in['Wss_q'], 'L0_xcond_bss_q': _L0_xcond_in['bss_q'], 'L0_xcond_Wss_kv': _L0_xcond_in['Wss_kv'], 'L0_xcond_bss_kv': _L0_xcond_in['bss_kv']}

def reference(x, ctx_1024, cond_1024, L0_xcond_Wq, L0_xcond_bq, L0_xcond_Wkv, L0_xcond_bkv, L0_xcond_Wp, L0_xcond_bp, L0_xcond_Wss_q, L0_xcond_bss_q, L0_xcond_Wss_kv, L0_xcond_bss_kv):
    import jax
    import jax.numpy as jnp

    def _L0_xcond_ref(x_q, x_kv, t_vec, Wq, bq, Wkv, bkv, Wp, bp, Wss_q, bss_q, Wss_kv, bss_kv):
        import jax, jax.numpy as jnp
        import numpy as np
        EPS = 1e-05

        def _ada_ln(x, c, W_ss, b_ss):
            mu = jnp.mean(x, axis=-1, keepdims=True)
            var = jnp.mean((x - mu) ** 2, axis=-1, keepdims=True)
            h = (x - mu) / jnp.sqrt(var + EPS)
            ss = jax.nn.silu(c) @ W_ss + b_ss
            scale, bias = jnp.split(ss, 2, axis=-1)
            return (1.0 + scale)[:, None, :] * h + bias[:, None, :]
        B, Lq, H = x_q.shape
        Lkv = x_kv.shape[1]
        nh = 16
        dh = H // nh
        xq = _ada_ln(x_q, t_vec, Wss_q, bss_q)
        xkv = _ada_ln(x_kv, t_vec, Wss_kv, bss_kv)
        q = (xq @ Wq + bq).reshape(B, Lq, nh, dh)
        kv = (xkv @ Wkv + bkv).reshape(B, Lkv, 2, nh, dh)
        k = kv[:, :, 0]
        v = kv[:, :, 1]
        scores = jnp.einsum('bqhd,bkhd->bhqk', q, k) / jnp.sqrt(jnp.float32(dh))
        attn = jax.nn.softmax(scores, axis=-1)
        out = jnp.einsum('bhqk,bkhd->bqhd', attn, v).reshape(B, Lq, H)
        return x_q + (out @ Wp + bp)
    x = _L0_xcond_ref(x, ctx_1024, cond_1024, L0_xcond_Wq, L0_xcond_bq, L0_xcond_Wkv, L0_xcond_bkv, L0_xcond_Wp, L0_xcond_bp, L0_xcond_Wss_q, L0_xcond_bss_q, L0_xcond_Wss_kv, L0_xcond_bss_kv)
    return x

_drawn_inputs = setup_inputs


def setup_inputs(seed=0):
    import zlib

    import numpy as np

    out = dict(_drawn_inputs(seed))
    spreads = {'L0_xcond_bq': (0.0, 2.0),
     'L0_xcond_bkv': (0.0, 0.1),
     'L0_xcond_bp': (0.0, 0.1),
     'L0_xcond_bss_q': (0.0, 0.8),
     'L0_xcond_bss_kv': (0.0, 0.354)}
    factors = {'L0_xcond_Wq': 6.683, 'L0_xcond_Wss_q': 8.0}
    for name, (base, spread) in spreads.items():
        noise = np.random.default_rng([zlib.crc32(name.encode()), seed]).standard_normal(out[name].shape)
        drawn = base * np.exp(spread * noise) if base else spread * noise
        out[name] = jnp.asarray(drawn.astype(out[name].dtype))
    for name, factor in factors.items():
        out[name] = (out[name] * factor).astype(out[name].dtype)
    return out
```

```python
from contextlib import ExitStack

import concourse.bass as bass
from concourse import mybir

P = 128
F32 = mybir.dt.float32
F32R = mybir.dt.float32r
I32 = mybir.dt.int32
ALU = mybir.AluOpType
ACT = mybir.ActivationFunctionType
AX_X = mybir.AxisListType.X
RMAX = bass.bass_isa.ReduceOp.max
ds = bass.ds

EPS = 1e-5
NH = 16
SHIFT_OK_SUM = 1e25
SHIFT_OK_RECIP = 1e20


def cross_attention(nc, x, ctx, cond, Wq, bq, Wkv, bkv, Wp, bp, Wss_q, bss_q, Wss_kv, bss_kv, out):
    _, LQ, H = x.shape
    LKV = ctx.shape[1]
    DH = H // NH
    FT = H // P
    HG = P // DH
    NG = NH // HG
    QB = 512
    NB = LQ // QB
    TPB = QB // P
    NT = LKV // P
    TAIL = LKV - NT * P
    CT = 5
    NC = NT // CT
    KB = -(-LKV // QB)
    KP = KB * QB
    RING = 3
    PR = 5
    ADDS = NT - 2
    LAST = NG - 1
    ITEMS = 2 * NT + 1
    UNITS = NG * NB
    SCALE = float(DH) ** -0.5
    SEL = P + TAIL
    assert DH == 32 and HG == 4 and TAIL * HG <= 32 and ITEMS % RING == 0 and NT % PR == 0 and NT % CT == 0
    assert LKV - (KB - 1) * QB == P + TAIL and NB % 2 == 0 and KB == NB - 1

    x2, ctx2, out2 = x[0], ctx[0], out[0]
    q_dram = nc.dram_tensor("q_split", [2, H, LQ], F32).ap()
    k_dram = nc.dram_tensor("k_split", [2, H, KP], F32).ap()
    v_dram = nc.dram_tensor("v_full", [KP, H], F32).ap()
    xt_dram = nc.dram_tensor("ctx_t", [H, KP], F32).ap()
    xb_dram = nc.dram_tensor("x_bias", [LQ, H], F32).ap()
    o_dram = nc.dram_tensor("o_sums", [H, LQ], F32).ap()
    l_dram = nc.dram_tensor("l_sums", [NH, LQ], F32).ap()
    r_dram = nc.dram_tensor("l_recip", [NH, LQ], F32).ap()

    START = 64

    def raise_to_start(eng, sems):
        for s in sems:
            eng.sem_inc(s, START)

    outer = ExitStack()
    flag = outer.enter_context(nc.sbuf_tensor("flag", [1, 1], I32))
    flag_ready = outer.enter_context(nc.semaphore("flag_ready"))

    def again(eng):
        eng.wait_ge(flag_ready, 1)
        return eng.If(eng.value_load(flag[0:1, 0:1], min_val=0, max_val=1))

    def prologue():
        with ExitStack() as st:
            def sb(name, shape, dt=F32):
                return st.enter_context(nc.sbuf_tensor(name, shape, dt))

            def sem(name):
                return st.enter_context(nc.semaphore(name))

            ident = sb("ident", [P, P])
            one1 = sb("one1", [1, 1])
            cond_c = sb("cond_c", [P, FT])
            silu_e = sb("silu_e", [P, FT])
            silu_d = sb("silu_d", [P, FT])
            silu_r = sb("silu_r", [P, FT])
            silu_c = sb("silu_c", [P, FT])
            wss = [sb(f"wss{i}", [P, FT, 2 * H]) for i in range(2)]
            bss = sb("bss", [1, 2, 2 * H])
            ss_row = sb("ss_row", [1, 2, 2 * H])
            mod = sb("mod", [P, 2, 2 * FT])
            wq = sb("wq", [P, FT, H])
            wk0 = sb("wk0", [P, FT, P])
            wv0 = sb("wv0", [P, FT, P])
            bq_c = sb("bq_c", [P, FT])
            bk_c = sb("bk_c", [P, FT])
            bv0_b = sb("bv0_b", [P, TPB, P])
            bp_b = sb("bp_b", [P, H])
            xin = [sb(f"xin{i}", [P, TPB, H]) for i in range(2)]
            hn = [sb(f"hn{i}", [P, TPB, H]) for i in range(2)]
            xt = [sb(f"xt{i}", [P, FT, QB]) for i in range(2)]
            hi = [sb(f"hi{i}", [P, FT, QB], F32R) for i in range(2)]
            lo = [sb(f"lo{i}", [P, FT, QB], F32R) for i in range(2)]
            vs = sb("vs", [P, TPB, P])
            xb = sb("xb", [P, TPB, H])
            stats = sb("stats", [P, TPB, 6])
            aggr = sb("aggr", [P, TPB, 2])
            var_eps = sb("var_eps", [P, TPB])
            minus_half = sb("minus_half", [P, TPB])
            rstd = sb("rstd", [P, TPB])
            bank = st.enter_context(nc.psum_tensor("bank", [P, 8, 512], F32))

            consts = sem("consts")
            cond_in = sem("cond_in")
            wss_in = sem("wss_in")
            weights_in = sem("weights_in")
            silu_step = sem("silu_step")
            ss_done = sem("ss_done")
            ss_rows = sem("ss_rows")
            ss_cols = sem("ss_cols")
            mod_ready = sem("mod_ready")
            x_in = [sem(f"x_in{i}") for i in range(2)]
            hi_ready = sem("hi_ready")
            rstd_ready = sem("rstd_ready")
            xb_ready = sem("xb_ready")
            wait_carrier = sem("wait_carrier")
            sp_carrier = sem("sp_carrier_p")
            stat_step = sem("stat_step")
            h_ready = sem("h_ready")
            t_ready = sem("t_ready")
            xt_ready = sem("xt_ready")
            proj_done = sem("proj_done")
            lo_ready = sem("lo_ready")
            v_ready = sem("v_ready")
            xb_out = sem("xb_out")
            xt_out = [sem(f"xt_out{i}") for i in range(2)]
            split_out = [sem(f"split_out{i}") for i in range(2)]
            v_out = sem("v_out")
            from_start = [stat_step, h_ready, t_ready, xt_ready, proj_done, lo_ready, v_ready, v_out, xb_out]
            from_start += split_out + xt_out

            class Blk:
                def __init__(self, half, off, kv, last=False):
                    self.half, self.off, self.kv, self.last = half, off, kv, last
                    self.n = 2 * half + off
                    self.par = off % 2
                    self.use = half + off // 2
                    self.splits = NB * FT + (self.n - NB) if kv else self.n * FT
                    self.results = NB * FT + 2 * (self.n - NB) if kv else self.n * FT
                    self.m_tiles = 1 if kv else FT

                def token0(self):
                    return (self.n - NB) * QB if self.kv else self.n * QB

            N_ALL = NB + KB

            def ahead(b, d):
                if isinstance(b.half, int):
                    n = b.n + d
                    return Blk(n // 2, n % 2, n >= NB, n == N_ALL - 1) if n < N_ALL else None
                return Blk(b.half, b.off + d, b.kv)

            def blocks(eng):
                with eng.Fori(0, NB // 2 - 1) as i:
                    yield Blk(i, 0, False)
                    yield Blk(i, 1, False)
                yield Blk(NB // 2 - 1, 0, False)
                yield Blk(NB // 2 - 1, 1, False)
                with eng.Fori(NB // 2, (N_ALL - 3) // 2) as i:
                    yield Blk(i, 0, True)
                    yield Blk(i, 1, True)
                for n in range(N_ALL - 3, N_ALL):
                    yield Blk(n // 2, n % 2, True, n == N_ALL - 1)

            with nc.Block() as block:
                @block.sync
                def _(sp):
                    sp.dma_start(cond_c[:, :], cond[0].rearrange("(t p) -> p t", p=P),
                                 allow_slow_non_contiguous=True).then_inc(cond_in, 16)
                    def load(b):
                        sp.wait_ge(h_ready, START + b.n - 1)
                        src = ctx2 if b.kv else x2
                        full = 1 if b.last else TPB
                        sp.dma_start(xin[b.par][:, 0:full, :],
                                     src[ds(b.token0(), P * full), :].rearrange("(j p) f -> p j f", p=P)
                                     ).then_inc(x_in[b.par], 16)
                        if b.last:
                            sp.dma_start(xin[b.par][0:TAIL, full, :], ctx2[NT * P:LKV, :]).then_inc(x_in[b.par], 16)

                    def store_residual(b):
                        sp.wait_ge(xb_ready, b.n + 1)
                        sp.dma_start(xb_dram[ds(b.token0(), QB), :].rearrange("(j p) f -> p j f", p=P),
                                     xb[:, :, :]).then_inc(xb_out, 16)

                    load(Blk(0, 0, False))
                    load(Blk(0, 1, False))
                    store_residual(Blk(0, 0, False))
                    for b in blocks(sp):
                        if ahead(b, 2):
                            load(ahead(b, 2))
                        if ahead(b, 1) and not ahead(b, 1).kv:
                            store_residual(ahead(b, 1))
                        cols = ds(b.token0(), QB)
                        if b.kv:
                            sp.wait_ge(xt_ready, START + FT * (b.n + 1))
                            sp.dma_start(xt_dram[:, cols].rearrange("(t p) q -> p t q", p=P),
                                         xt[b.par][:, :, :]).then_inc(xt_out[b.par], 16)
                        dst = (k_dram if b.kv else q_dram)[:, 0:b.m_tiles * P, :]
                        sp.wait_ge(lo_ready, START + b.splits + b.m_tiles)
                        sp.sem_inc(sp_carrier, 1)
                        for part, tile in ((0, hi), (1, lo)):
                            sp.dma_start(dst[part, :, cols].rearrange("(t p) q -> p t q", p=P),
                                         tile[b.par][:, 0:b.m_tiles, :].bitcast(F32)).then_inc(split_out[b.par], 16)
                        if b.kv:
                            sp.wait_ge(v_ready, START + b.n - NB + 1)
                            sp.dma_start(v_dram[cols, 0:P].rearrange("(j p) f -> p j f", p=P),
                                         vs[:, :, :]).then_inc(v_out, 16)
                    for par in range(2):
                        sp.wait_ge(split_out[par], START + 32 * ((N_ALL + 1 - par) // 2))
                        sp.wait_ge(xt_out[par], START + 16 * ((KB + 1 - par) // 2))
                    sp.wait_ge(v_out, START + 16 * KB)
                    sp.wait_ge(xb_out, START + 16 * NB)

                @block.gpsimd
                def _(pool):
                    raise_to_start(pool, from_start)
                    nc.gpsimd.memset(ident[:, :], 0.0).then_inc(consts, 1)
                    nc.gpsimd.memset(one1[:, :], 1.0).then_inc(consts, 1)
                    nc.gpsimd.memset(minus_half[:, :], -0.5).then_inc(consts, 1)
                    pool.wait_ge(consts, 3)
                    nc.gpsimd.affine_select(out=ident[:, :], in_=ident[:, :], compare_op=ALU.not_equal, fill=1.0,
                                            base=0, pattern=[[-1, P]], channel_multiplier=1).then_inc(consts, 1)

                    def inverse_deviation(b):
                        pool.wait_ge(stat_step, START + 3 * (b.n + 1))
                        nc.gpsimd.tensor_tensor(rstd[:, :], var_eps[:, :], minus_half[:, :],
                                                ALU.pow).then_inc(rstd_ready, 1)

                    inverse_deviation(Blk(0, 0, False))
                    inverse_deviation(Blk(0, 1, False))
                    for b in blocks(pool):
                        if ahead(b, 2):
                            inverse_deviation(ahead(b, 2))

                @block.tensor
                def _(pe):
                    pe.wait_ge(wss_in, 64)
                    pe.wait_ge(silu_step, 4)
                    for w in range(2):
                        for half in range(2):
                            for k in range(FT):
                                mm = nc.tensor.matmul(bank[0:1, 2 * w + half, :], silu_c[:, k:k + 1],
                                                      wss[w][:, k, half * H:(half + 1) * H],
                                                      start=(k == 0), stop=(k == FT - 1))
                    mm.then_inc(ss_done, 1)
                    pe.wait_ge(consts, 4)
                    pe.wait_ge(ss_rows, 1)
                    for w in range(2):
                        for c in range(2 * FT):
                            col = 2 * FT * w + c
                            mm = nc.tensor.matmul(bank[:, 4, col:col + 1], ss_row[0:1, w, c * P:(c + 1) * P],
                                                  one1[0:1, 0:1], start=True, stop=True)
                    mm.then_inc(ss_cols, 1)

                    def transposes(b):
                        pe.wait_ge(h_ready, START + b.n + 1)
                        for f in range(FT):
                            pe.wait_ge(xt_ready, START + FT * (b.n - 1) + f + 1)
                            for j in range(TPB):
                                mm = nc.tensor.transpose(bank[:, f, j * P:(j + 1) * P],
                                                         hn[b.par][:, j, f * P:(f + 1) * P], ident[:, :])
                            mm.then_inc(t_ready, 1)

                    pe.wait_ge(weights_in, 16 * (5 + TPB + 1))
                    pe.wait_ge(mod_ready, 1)
                    transposes(Blk(0, 0, False))
                    for b in blocks(pe):
                        if ahead(b, 1):
                            transposes(ahead(b, 1))
                        pe.wait_ge(xt_ready, START + FT * (b.n + 1))
                        if not b.kv:
                            for m in range(FT):
                                pe.wait_ge(lo_ready, START + FT * (b.n - 1) + m + 1)
                                for k in range(FT):
                                    mm = nc.tensor.matmul(bank[:, 4 + m, :], wq[:, k, m * P:(m + 1) * P],
                                                          xt[b.par][:, k, :], start=(k == 0), stop=(k == FT - 1))
                                mm.then_inc(proj_done, 1)
                        else:
                            pe.wait_ge(lo_ready, START + b.splits - 1)
                            pe.wait_ge(v_ready, START + b.n - NB - 1)
                            for k in range(FT):
                                mm = nc.tensor.matmul(bank[:, 4 + 2 * b.par, :], wk0[:, k, :], xt[b.par][:, k, :],
                                                      start=(k == 0), stop=(k == FT - 1))
                            mm.then_inc(proj_done, 1)
                            for j in range(TPB):
                                for k in range(FT):
                                    mm = nc.tensor.matmul(bank[:, 5 + 2 * b.par, j * P:(j + 1) * P],
                                                          xt[b.par][:, k, j * P:(j + 1) * P], wv0[:, k, :],
                                                          start=(k == 0), stop=(k == FT - 1))
                            mm.then_inc(proj_done, 1)

                @block.scalar
                def _(act):
                    for w, (weight, bias) in enumerate(((Wss_q, bss_q), (Wss_kv, bss_kv))):
                        act.dma_start(bss[:, w, :], bias.rearrange("(a n) -> a n", a=1)).then_inc(wss_in, 16)
                        act.dma_start(wss[w][:, :, :], weight.rearrange("(t p) n -> p t n", p=P)).then_inc(wss_in, 16)
                    act.dma_start(wq[:, :, :], Wq.rearrange("(t p) n -> p t n", p=P)).then_inc(weights_in, 16)
                    act.dma_start(bq_c[:, :], bq.rearrange("(t p) -> p t", p=P),
                                  allow_slow_non_contiguous=True).then_inc(weights_in, 16)
                    for w, col in ((wk0, 0), (wv0, H)):
                        act.dma_start(w[:, :, :],
                                      Wkv[:, col:col + P].rearrange("(t p) n -> p t n", p=P)).then_inc(weights_in, 16)
                    act.dma_start(bk_c[:, :], bkv[0:H].rearrange("(t p) -> p t", p=P),
                                  allow_slow_non_contiguous=True).then_inc(weights_in, 16)
                    for j in range(TPB):
                        act.dma_start(bv0_b[:, j, :], bkv[H:H + P].rearrange("(a n) -> a n", a=1)
                                      .broadcast_to([P, P])).then_inc(weights_in, 16)
                    act.dma_start(bp_b[:, :], bp.rearrange("(a n) -> a n", a=1)
                                  .broadcast_to([P, H])).then_inc(weights_in, 16)
                    act.wait_ge(cond_in, 16)
                    nc.scalar.activation(silu_e[:, :], cond_c[:, :], ACT.Exp, scale=-1.0).then_inc(silu_step, 1)

                    def modulate(b):
                        first_kv = isinstance(b.n, int) and b.n == NB
                        act.wait_ge(proj_done, START + b.results - (2 if b.kv and not first_kv else FT))
                        if b.kv:
                            act.wait_ge(xt_out[b.par], START + 16 * (b.use - NB // 2))
                        w = 1 if b.kv else 0
                        for f in range(FT):
                            act.wait_ge(t_ready, START + FT * b.n + f + 1)
                            nc.scalar.activation(xt[b.par][:, f, :], bank[:, f, :], ACT.Identity,
                                                 scale=mod[:, w, f:f + 1],
                                                 bias=mod[:, w, FT + f:FT + f + 1]).then_inc(xt_ready, 1)

                    act.wait_ge(mod_ready, 1)
                    act.wait_ge(weights_in, 16 * (5 + TPB + 1))
                    modulate(Blk(0, 0, False))
                    for b in blocks(act):
                        if ahead(b, 1):
                            modulate(ahead(b, 1))
                        bias = bk_c if b.kv else bq_c
                        act.wait_ge(split_out[b.par], START + 32 * b.use)
                        for m in range(b.m_tiles):
                            act.wait_ge(proj_done, START + b.results + m + 1)
                            src = bank[:, 4 + (2 * b.par if b.kv else m), :]
                            nc.scalar.activation(hi[b.par][:, m, :], src, ACT.Identity,
                                                 bias=bias[:, m:m + 1]).then_inc(hi_ready, 1)

                @block.vector
                def _(dve):
                    dve.wait_ge(silu_step, 1)
                    nc.vector.tensor_scalar_add(silu_d[:, :], silu_e[:, :], 1.0).then_inc(silu_step, 1)
                    dve.wait_ge(silu_step, 2)
                    nc.vector.reciprocal(silu_r[:, :], silu_d[:, :]).then_inc(silu_step, 1)
                    dve.wait_ge(silu_step, 3)
                    nc.vector.tensor_tensor(silu_c[:, :], silu_r[:, :], cond_c[:, :], ALU.mult).then_inc(silu_step, 1)

                    def normalise(b):
                        tiles = range(TPB)
                        dve.wait_ge(x_in[b.par], 16 * (b.use + 1) + (16 if b.last else 0))
                        dve.wait_ge(t_ready, START + FT * (b.n - 1))
                        for j in tiles:
                            i = nc.vector.bn_stats(stats[:, j, :], xin[b.par][:, j, :])
                        i.then_inc(stat_step, 1)
                        dve.wait_ge(stat_step, START + 3 * b.n + 1)
                        dve.sem_inc(wait_carrier, 1)
                        for j in tiles:
                            i = nc.vector.bn_aggr(aggr[:, j, :], stats[:, j, :])
                        i.then_inc(stat_step, 1)
                        dve.wait_ge(stat_step, START + 3 * b.n + 2)
                        nc.vector.tensor_scalar_add(var_eps[:, :], aggr[:, :, 1], EPS).then_inc(stat_step, 1)
                        if not b.kv:
                            dve.wait_ge(xb_out, START + 16 * b.n)
                            for j in tiles:
                                i = nc.vector.tensor_tensor(xb[:, j, :], xin[b.par][:, j, :], bp_b[:, :], ALU.add)
                            i.then_inc(xb_ready, 1)
                        dve.wait_ge(rstd_ready, b.n + 1)
                        for j in tiles:
                            i = nc.vector.tensor_scalar(hn[b.par][:, j, :], xin[b.par][:, j, :], aggr[:, j, 0:1],
                                                        rstd[:, j:j + 1], ALU.subtract, ALU.mult)
                        i.then_inc(h_ready, 1)

                    dve.wait_ge(weights_in, 16 * (5 + TPB + 1))
                    normalise(Blk(0, 0, False))
                    normalise(Blk(0, 1, False))
                    dve.wait_ge(ss_done, 1)
                    dve.wait_ge(wss_in, 64)
                    nc.vector.tensor_tensor(ss_row[0:1, :, :].rearrange("p w n -> p (w n)"),
                                            bank[0:1, 0:4, :].rearrange("p a n -> p (a n)"),
                                            bss[0:1, :, :].rearrange("p w n -> p (w n)"),
                                            ALU.add).then_inc(ss_rows, 1)
                    dve.wait_ge(ss_cols, 1)
                    cols = bank[:, 4, 0:4 * FT].rearrange("p (w c) -> p w c", w=2)
                    nc.vector.tensor_scalar_add(mod[:, :, 0:FT], cols[:, :, 0:FT], 1.0)
                    nc.vector.tensor_copy(mod[:, :, FT:2 * FT], cols[:, :, FT:2 * FT]).then_inc(mod_ready, 1)
                    
                    for b in blocks(dve):
                        if ahead(b, 2):
                            normalise(ahead(b, 2))
                        bias = bk_c if b.kv else bq_c
                        for m in range(b.m_tiles):
                            dve.wait_ge(hi_ready, b.splits + m + 1)
                            src = bank[:, 4 + (2 * b.par if b.kv else m), :]
                            nc.vector.scalar_tensor_tensor(out=lo[b.par][:, m, :], in0=src, scalar=bias[:, m:m + 1],
                                                           in1=hi[b.par][:, m, :].bitcast(F32),
                                                           op0=ALU.add, op1=ALU.subtract).then_inc(lo_ready, 1)
                        if b.kv:
                            dve.wait_ge(v_out, START + 16 * (b.n - NB))
                            dve.wait_ge(proj_done, START + b.results + 2)
                            nc.vector.tensor_tensor(vs[:, :, :].rearrange("p j f -> p (j f)"), bank[:, 5 + 2 * b.par, :],
                                                    bv0_b[:, :, :].rearrange("p j f -> p (j f)"),
                                                    ALU.add).then_inc(v_ready, 1)

    def attention_and_check():
        with ExitStack() as st:
            def sb(name, shape, dt=F32):
                return st.enter_context(nc.sbuf_tensor(name, shape, dt))

            def sem(name):
                return st.enter_context(nc.semaphore(name))

            ks = sb("ks", [P, HG, NT * P], F32R)
            kt = sb("kt", [P, HG * SEL], F32R)
            vg = sb("vg", [P, NT, P])
            vt = sb("vt", [TAIL * HG, P])
            qs = [sb(f"qs{i}", [P, HG, QB], F32R) for i in range(2)]
            pt = [sb(f"pt{i}", [P, HG, QB]) for i in range(PR)]
            pt_tail = [sb(f"pt_tail{i}", [TAIL * HG, QB]) for i in range(2)]
            acc = [[sb(f"acc{i}{a}", [P, HG, QB]) for a in "ab"] for i in range(2)]
            o_sb = sb("o_sb", [P, QB])
            l_sb = sb("l_sb", [P, QB])
            ones = sb("ones", [P, DH])
            ones_blk = sb("ones_blk", [TAIL * HG, P])
            zero_bias = sb("zero_bias", [P, 1])
            s_max = sb("s_max", [P, 1])
            g_max = sb("g_max", [P, 1])
            shift = sb("shift", [P, 1])
            l_blk = sb("l_blk", [P, NH * QB // P])
            r_blk = sb("r_blk", [P, NH * QB // P])
            l_top = sb("l_top", [P, 2])
            l_ok = sb("l_ok", [P, 3])

            W5 = H * 4
            work = sb("work", [P, 5 * W5])
            xt = work[:, 0:W5].rearrange("p (t q) -> p t q", t=FT)
            wk = work[:, W5:W5 + H].rearrange("p (t n) -> p t n", t=FT)
            wv = work[:, W5 + H:W5 + 2 * H].rearrange("p (t n) -> p t n", t=FT)
            bk_c = work[:, 2 * W5 - 1:2 * W5]
            bv_b = work[:, W5 + 2 * H:W5 + 3 * H].rearrange("p (j n) -> p j n", j=TPB)
            k_hi = work[:, 2 * W5:2 * W5 + H]
            k_lo = work[:, 2 * W5 + H:2 * W5 + 2 * H]
            v_st = work[:, 2 * W5 + 2 * H:2 * W5 + 3 * H].rearrange("p (j n) -> p j n", j=TPB)

            def quarter(i):
                return work[:, i * W5:(i + 1) * W5].rearrange("p (g q) -> p g q", g=NG)

            wp, o_in, r_b, on, xy = (quarter(i) for i in range(5))
            l_all = work[:, W5:W5 + NH * LQ // P]
            r_all = work[:, 2 * W5:2 * W5 + NH * LQ // P]
            m_row = work[0:1, 0:W5].rearrange("p (h q) -> p h q", h=HG)
            row_tail = work[0:1, W5:W5 + HG * SEL]
            row1 = work[0:1, 2 * W5:2 * W5 + P]
            ident = work[:, 3 * W5:3 * W5 + P]
            m_part = work[:, 4 * W5:4 * W5 + 3 * HG * TPB].rearrange("p (c k) -> p c k", k=3)
            m_col = work[:, 4 * W5 + H:4 * W5 + H + HG * TPB]
            ring = st.enter_context(nc.psum_tensor("ring", [P, 2 * RING, 512], F32))
            o_ps = st.enter_context(nc.psum_tensor("o_ps", [P, 512], F32))
            l_ps = st.enter_context(nc.psum_tensor("l_ps", [P, 512], F32))

            consts = sem("consts_a")
            fills = sem("fills")
            exact_consts = sem("exact_consts")
            k_in = [sem(f"k_in{c}") for c in range(NC)]
            tail_in = sem("tail_in")
            q_in = [sem(f"q_in{i}") for i in range(2)]
            s_ready = sem("s_ready")
            e_done = sem("e_done")
            sample_ready = sem("sample_ready")
            sample_max = sem("sample_max")
            wait_carrier = sem("wait_carrier_a")
            sp_carrier = sem("sp_carrier")
            shift_ready = sem("shift_ready")
            task_w_in = sem("task_w_in")
            xt_in = sem("xt_in")
            hi_done = sem("hi_done")
            rows_ready = sem("rows_ready")
            m_ready = sem("m_ready")
            m_turned = sem("m_turned")
            m_rows = sem("m_rows")
            wp_in = sem("wp_in")
            l_blk_in = sem("l_blk_in")
            r_blk_done = sem("r_blk_done")
            r_blk_out = sem("r_blk_out")
            or_in = sem("or_in")
            xy_in = [sem(f"xy_in{i}") for i in range(2)]
            y_done = sem("y_done")
            l_step = sem("l_step")
            l_in = sem("l_in")
            r_out = sem("r_out")
            r_ready = sem("r_ready")
            flag_sum = sem("flag_sum")
            pv_done = sem("pv_done")
            p_added = sem("p_added")
            o_ready = sem("o_ready")
            o_taken = sem("o_taken")
            l_ready = sem("l_ready")
            l_taken = sem("l_taken")
            group_max = sem("group_max")
            rows_taken = sem("rows_taken")
            o_out = sem("o_out")
            l_out = sem("l_out")
            kv_ready = sem("kv_ready")
            lo_done = sem("lo_done")
            v_done = sem("v_done")
            k_out = sem("k_out")
            v_out = sem("v_out_a")
            on_ready = sem("on_ready")
            y_added = sem("y_added")
            y_out = [sem(f"y_out{i}") for i in range(2)]
            from_start = [pv_done, p_added, o_ready, o_taken, l_ready, l_taken, group_max, rows_taken, o_out, l_out,
                          kv_ready, lo_done, v_done, k_out, v_out, on_ready, y_added] + y_out

            AT_L = PR + 2
            AT_K, AT_V = 10, 17
            AT_Y = (0, 10, 15, 20)
            AT_SAMPLE = 18

            class Unit:
                def __init__(self, G, half, par):
                    self.G, self.par = G, par
                    self.b = 2 * half + par
                    self.u = G * NB + self.b
                    self.use = G * (NB // 2) + half
                    self.starts_group = isinstance(half, int) and half == 0 and par == 0

            def groups(eng):
                yield 0
                with eng.Fori(1, LAST) as g:
                    yield g

            def scores_done(U, n):
                return U.u * ITEMS + n + 1

            def add_of(t):
                return max(t - 1, 1) if t < 2 or t > 3 else 2

            def tail_of(t, h):
                return t[:, h * P:(h + 1) * P]

            def load_q(sp, g, U):
                sp.wait_ge(o_ready, START + U.u - 1)
                for r in range(4):
                    src = q_dram[r % 2, ds(g * P, P), ds(U.b * QB, QB)].rearrange("(h d) q -> d h q", d=DH)
                    sp.dma_start(qs[U.par][r * DH:(r + 1) * DH, :, :].bitcast(F32), src).then_inc(q_in[U.par], 16)

            def load_keys(sp, g, G):
                for c in range(NC):
                    sp.wait_ge(pv_done, START + (G * NB - 1) * NT + CT * (c + 1))
                    keys = slice(c * CT * P, (c + 1) * CT * P)
                    for r in range(4):
                        src = k_dram[r // 2, ds(g * P, P), keys].rearrange("(h d) k -> d h k", d=DH)
                        sp.dma_start(ks[r * DH:(r + 1) * DH, :, keys].bitcast(F32), src).then_inc(k_in[c], 16)
                    sp.dma_start(vg[:, c * CT:(c + 1) * CT, :],
                                 v_dram[keys, ds(g * P, P)].rearrange("(t p) n -> p t n", p=P)).then_inc(k_in[c], 16)

            def load_tail(sp, g, G):
                sp.wait_ge(o_ready, START + G * NB)
                for r in range(4):
                    src = k_dram[r // 2, ds(g * P, P), NT * P:LKV].rearrange("(h d) k -> d h k", d=DH)
                    dst = kt[r * DH:(r + 1) * DH, :].rearrange("p (h c) -> p h c", c=SEL)[:, :, 0:TAIL]
                    sp.dma_start(dst.bitcast(F32), src).then_inc(tail_in, 16)
                for h in range(HG):
                    sp.dma_start(vt[TAIL * h:TAIL * (h + 1), h * DH:(h + 1) * DH],
                                 v_dram[NT * P:LKV, ds(g * P + h * DH, DH)]).then_inc(tail_in, 16)

            def store_o(sp, g, U):
                sp.wait_ge(o_taken, START + U.u + 1)
                sp.dma_start(o_dram[ds(g * P, P), ds(U.b * QB, QB)], o_sb[:, :]).then_inc(o_out, 16)

            def store_l(sp, g, U):
                sp.wait_ge(l_taken, START + U.u + 1)
                sp.dma_start(l_dram[ds(g * HG, HG), ds(U.b * QB, QB)], l_sb[0:P:DH, :]).then_inc(l_out, 16)

            def load_task_weights(sp, g):
                sp.wait_ge(v_done, START + KB * g)
                for w, col in ((wk, 0), (wv, H)):
                    sp.dma_start(w, Wkv[:, ds((g + 1) * P + col, P)].rearrange("(t p) n -> p t n", p=P)
                                 ).then_inc(task_w_in, 16)
                sp.dma_start(bk_c, bkv[ds((g + 1) * P, P)].rearrange("(p a) -> p a", a=1)).then_inc(task_w_in, 16)
                for j in range(TPB):
                    sp.dma_start(bv_b[:, j, :], bkv[ds((g + 1) * P + H, P)].rearrange("(a n) -> a n", a=1)
                                 .broadcast_to([P, P])).then_inc(task_w_in, 16)

            TASK_W = 16 * (3 + TPB)

            class Task:
                def __init__(self, g, b):
                    self.g, self.b = g, b
                    self.t = g * KB + b

            def load_xt(sp, T):
                sp.wait_ge(kv_ready, START + 2 * T.t)
                sp.sem_inc(sp_carrier, 1)
                sp.dma_start(xt, xt_dram[:, ds(T.b * QB, QB)].rearrange("(t p) q -> p t q", p=P)).then_inc(xt_in, 16)

            def store_task(sp, T):
                cols = ds(T.b * QB, QB)
                rows = ds((T.g + 1) * P, P)
                sp.wait_ge(lo_done, START + T.t + 1)
                sp.dma_start(k_dram[0, rows, cols], k_hi).then_inc(k_out, 16)
                sp.dma_start(k_dram[1, rows, cols], k_lo).then_inc(k_out, 16)
                sp.wait_ge(v_done, START + T.t + 1)
                sp.dma_start(v_dram[cols, rows].rearrange("(j p) f -> p j f", p=P), v_st).then_inc(v_out, 16)

            def load_xy(sp, b, half):
                sp.wait_ge(y_out[half], START + 16 * b)
                sp.dma_start(xy[:, 2 * half:2 * half + 2, :],
                             xb_dram[ds(b * QB + 2 * half * P, 2 * P), :].rearrange("(j p) f -> p j f", p=P)
                             ).then_inc(xy_in[half], 16)

            def store_y(sp, b, half):
                sp.wait_ge(y_added, START + TPB * b + 2 * half + 2)
                sp.dma_start(out2[ds(b * QB + 2 * half * P, 2 * P), :].rearrange("(j p) f -> p j f", p=P),
                             xy[:, 2 * half:2 * half + 2, :]).then_inc(y_out[half], 16)

            def prepare_block(sp, b):
                cols = ds(b * QB, QB)
                U = Unit(LAST, 0, 0)
                sp.wait_ge(l_out, START + 16 * (U.u + b + 1))
                flat = l_dram[:, cols].rearrange("h (a q) -> h a q", a=P // NH)
                sp.dma_start(l_blk[:, :], flat).then_inc(l_blk_in, 16)
                sp.wait_ge(r_blk_done, b + 1)
                sp.dma_start(r_dram[:, cols].rearrange("h (a q) -> h a q", a=P // NH), r_blk[:, :]
                             ).then_inc(r_blk_out, 16)
                sp.wait_ge(o_out, START + 16 * (U.u + b + 1))
                sp.wait_ge(on_ready, START + b)
                sp.dma_start(o_in, o_dram[:, cols].rearrange("(g p) q -> p g q", p=P)).then_inc(or_in, 16)
                sp.wait_ge(r_blk_out, 16 * (b + 1))
                for j in range(HG):
                    src = r_dram[:, cols].rearrange("(g j) q -> j g q", j=HG)[j:j + 1, :, :]
                    sp.dma_start(r_b[j * DH:(j + 1) * DH, :, :], src.broadcast_to([DH, NG, QB])).then_inc(or_in, 16)

            def transfers(sp):
                load_q(sp, 0, Unit(0, 0, 0))
                load_keys(sp, 0, 0)
                for g in groups(sp):
                    load_tail(sp, g, g)
                    load_task_weights(sp, g)
                    load_q(sp, g, Unit(g, 0, 1))
                    load_xt(sp, Task(g, 0))
                    if not isinstance(g, int):
                        store_o(sp, g - 1, Unit(g - 1, NB // 2 - 1, 1))
                        store_l(sp, g - 1, Unit(g - 1, NB // 2 - 1, 1))
                    store_task(sp, Task(g, 0))

                    def unit(U, prev, nxt):
                        load_q(sp, g, nxt)
                        load_xt(sp, Task(g, U.b))
                        store_o(sp, g, prev)
                        store_l(sp, g, prev)
                        store_task(sp, Task(g, U.b))

                    with sp.Fori(1, NB // 2) as half:
                        unit(Unit(g, half - 1, 1), Unit(g, half - 1, 0), Unit(g, half, 0))
                        unit(Unit(g, half, 0), Unit(g, half - 1, 1), Unit(g, half, 1))
                    load_q(sp, g + 1, Unit(g + 1, 0, 0))
                    store_o(sp, g, Unit(g, NB // 2 - 1, 0))
                    store_l(sp, g, Unit(g, NB // 2 - 1, 0))
                    sp.wait_ge(k_out, START + 32 * KB * (g + 1))
                    sp.wait_ge(v_out, START + 16 * KB * (g + 1))
                    load_keys(sp, g + 1, g + 1)

                U = [Unit(LAST, b // 2, b % 2) for b in range(NB)]
                load_tail(sp, LAST, LAST)
                load_q(sp, LAST, U[1])
                store_o(sp, LAST - 1, Unit(LAST - 1, NB // 2 - 1, 1))
                store_l(sp, LAST - 1, Unit(LAST - 1, NB // 2 - 1, 1))
                sp.dma_start(wp, Wp.rearrange("(g p) n -> p g n", p=P)).then_inc(wp_in, 16)
                load_q(sp, LAST, U[2])
                store_o(sp, LAST, U[0])
                store_l(sp, LAST, U[0])
                prepare_block(sp, 0)
                load_xy(sp, 0, 0)
                for b in range(2, NB):
                    if b + 1 < NB:
                        load_q(sp, LAST, U[b + 1])
                    load_xy(sp, b - 2, 1)
                    store_o(sp, LAST, U[b - 1])
                    store_l(sp, LAST, U[b - 1])
                    prepare_block(sp, b - 1)
                    store_y(sp, b - 2, 0)
                    load_xy(sp, b - 1, 0)
                    store_y(sp, b - 2, 1)
                load_xy(sp, NB - 2, 1)
                store_o(sp, LAST, U[NB - 1])
                store_l(sp, LAST, U[NB - 1])
                prepare_block(sp, NB - 1)
                for b in (NB - 2, NB - 1):
                    store_y(sp, b, 0)
                    if b + 1 < NB:
                        load_xy(sp, b + 1, 0)
                    store_y(sp, b, 1)
                    if b + 1 < NB:
                        load_xy(sp, b + 1, 1)
                for half in range(2):
                    sp.wait_ge(y_out[half], START + 16 * NB)

            def exact_transfers(sp):
                with sp.Fori(0, NG) as g:
                    G = g + NG
                    load_q(sp, g, Unit(G, 0, 0))
                    load_keys(sp, g, G)
                    load_tail(sp, g, G)
                    load_q(sp, g, Unit(G, 0, 1))
                    store_o(sp, g, Unit(G, 0, 0))
                    store_l(sp, g, Unit(G, 0, 0))
                    with sp.Fori(1, NB // 2) as half:
                        load_q(sp, g, Unit(G, half, 0))
                        store_o(sp, g, Unit(G, half - 1, 1))
                        store_l(sp, g, Unit(G, half - 1, 1))
                        load_q(sp, g, Unit(G, half, 1))
                        store_o(sp, g, Unit(G, half, 0))
                        store_l(sp, g, Unit(G, half, 0))
                    store_o(sp, g, Unit(G, NB // 2 - 1, 1))
                    store_l(sp, g, Unit(G, NB // 2 - 1, 1))

            def load_sums(sp, runs):
                sp.wait_ge(l_out, START + 16 * runs * UNITS)
                sp.wait_ge(o_out, START + 16 * runs * UNITS)
                sp.wait_ge(on_ready, START + NB)
                sp.dma_start(l_all, l_dram.rearrange("h (a q) -> (h a) q", a=P // NH)).then_inc(l_in, 16)

            def store_reciprocals(sp):
                sp.wait_ge(r_ready, 2)
                sp.dma_start(r_dram.rearrange("h (a q) -> (h a) q", a=P // NH), r_all).then_inc(r_out, 16)
                sp.wait_ge(r_out, 16)

            def sample_maxima(pool):
                with pool.Fori(0, NG) as G:
                    pool.wait_ge(sample_max, G + 1)
                    pool.sem_inc(wait_carrier, 1)
                    nc.gpsimd.partition_all_reduce(g_max[:, :], s_max[:, :], P, RMAX).then_inc(group_max, 1)

            def pe_run(pe, first_G, exact):
                def scores(U, n, first):
                    bank = 2 * (n % RING)
                    if n >= RING:
                        pe.wait_ge(e_done, scores_done(U, n - RING))
                    elif not first:
                        pe.wait_ge(e_done, U.u * ITEMS + n - RING + 1)
                        if n == 0 and U.starts_group:
                            pe.wait_ge(k_in[0], 80 * (U.G + 1))
                    if n == 0:
                        pe.wait_ge(q_in[U.par], 64 * (U.use + 1))
                    if n == ITEMS - 1:
                        if U.starts_group and not exact:
                            pe.wait_ge(tail_in, 128 * (U.G + 1))
                        for h in range(HG):
                            mm = nc.tensor.matmul(ring[:, bank, :], tail_of(kt, h), qs[U.par][:, h, :],
                                                  start=(h == 0), stop=(h == HG - 1 and not exact))
                        if exact:
                            for h in range(HG):
                                mm = nc.tensor.matmul(ring[:, bank, :], tail_of(row_tail, h), m_row[0:1, h, :],
                                                      start=False, stop=(h == HG - 1))
                    else:
                        t, pair = divmod(n, 2)
                        if U.starts_group and not exact and pair == 0 and t % CT == 0 and t > 0:
                            pe.wait_ge(k_in[t // CT], 80 * (U.G + 1))
                        for i in range(2):
                            h = 2 * pair + i
                            mm = nc.tensor.matmul(ring[:, bank + i, :], ks[:, h, t * P:(t + 1) * P],
                                                  qs[U.par][:, h, :], start=True, stop=not exact)
                            if exact:
                                mm = nc.tensor.matmul(ring[:, bank + i, :], row1[0:1, :], m_row[0:1, h, :],
                                                      start=False, stop=True)
                    mm.then_inc(s_ready, 1)

                def weigh(U, t):
                    pe.wait_ge(e_done, scores_done(U, 2 * t + 1))
                    if t == 0:
                        pe.wait_ge(o_taken, START + U.u)
                    for h in range(HG):
                        cols = slice(h * DH, (h + 1) * DH)
                        mm = nc.tensor.matmul(o_ps[cols, :], vg[:, t, cols], pt[t % PR][:, h, :],
                                              start=(t == 0), stop=False, skip_group_check=True)
                    mm.then_inc(pv_done, 1)

                def weigh_tail(U):
                    pe.wait_ge(e_done, scores_done(U, ITEMS - 1))
                    nc.tensor.matmul(o_ps[:, :], vt[:, :], pt_tail[U.par][:, :], start=False, stop=True,
                                     skip_group_check=True).then_inc(o_ready, 1)

                def denominators(U):
                    pe.wait_ge(p_added, START + ADDS * (U.u + 1))
                    pe.wait_ge(l_taken, START + U.u)
                    for a in range(2):
                        for h in range(HG):
                            nc.tensor.matmul(l_ps[h * DH:(h + 1) * DH, :], ones[:, :], acc[U.par][a][:, h, :],
                                             start=(a == 0), stop=False, skip_group_check=True)
                    nc.tensor.matmul(l_ps[:, :], ones_blk[:, :], pt_tail[U.par][:, :], start=False, stop=True,
                                     skip_group_check=True).then_inc(l_ready, 1)

                def unit(U, nxt, side):
                    for t in range(NT):
                        for n in (2 * t + RING, 2 * t + RING + 1):
                            if n < ITEMS:
                                scores(U, n, exact)
                            elif nxt is not None:
                                scores(nxt, n - ITEMS, False)
                        weigh(U, t)
                        side(t)
                    if nxt is not None:
                        scores(nxt, RING - 1, False)
                    weigh_tail(U)

                def sample(G):
                    pe.wait_ge(q_in[0], 64 * (Unit(G, 0, 0).use + 1))
                    pe.wait_ge(k_in[0], 80 * (G + 1))
                    pe.wait_ge(l_taken, START + Unit(G, 0, 0).u - 1)
                    for h in range(HG):
                        mm = nc.tensor.matmul(l_ps[:, h * P:(h + 1) * P], ks[:, h, 0:P], qs[0][:, h, 0:P],
                                              start=True, stop=True)
                    mm.then_inc(sample_ready, 1)

                def project(T, t):
                    k = t - AT_K
                    if k == 0:
                        pe.wait_ge(task_w_in, TASK_W * (T.g + 1))
                        pe.wait_ge(xt_in, 16 * (T.t + 1))
                        pe.wait_ge(l_taken, START + T.g * NB + T.b)
                    if 0 <= k < FT:
                        mm = nc.tensor.matmul(l_ps[:, :], wk[:, k, :], xt[:, k, :], start=(k == 0), stop=(k == FT - 1))
                        if k == FT - 1:
                            mm.then_inc(kv_ready, 1)
                    j = t - AT_V
                    if j == 0:
                        pe.wait_ge(lo_done, START + T.t + 1)
                    if 0 <= j < TPB:
                        for k in range(FT):
                            mm = nc.tensor.matmul(l_ps[:, j * P:(j + 1) * P], xt[:, k, j * P:(j + 1) * P], wv[:, k, :],
                                                  start=(k == 0), stop=(k == FT - 1))
                        if j == TPB - 1:
                            mm.then_inc(kv_ready, 1)

                def output_step(b, j, g, bank):
                    if g == 0:
                        if b == 0 and j == 0:
                            pe.wait_ge(wp_in, 16)
                        pe.wait_ge(on_ready, START + b + 1)
                    mm = nc.tensor.matmul(bank, on[:, g, j * P:(j + 1) * P], wp[:, g, :],
                                          start=(g == 0), stop=(g == NG - 1))
                    if g == NG - 1:
                        mm.then_inc(y_done, 1)

                def row_maxima(U, v):
                    pe.wait_ge(q_in[U.par], 64 * (U.use + 1))
                    for c in range(NC):
                        pe.wait_ge(k_in[c], 80 * (U.G + 1))
                    pe.wait_ge(tail_in, 128 * (U.G + 1))
                    pe.wait_ge(o_taken, START + U.u)
                    pe.wait_ge(exact_consts, 4 + HG)
                    chunks = [slice(c * 512, min((c + 1) * 512, NT * P)) for c in range((NT * P + 511) // 512)]
                    for hs in range(HG * TPB):
                        h, sub = divmod(hs, TPB)
                        q = qs[U.par][:, h, sub * P:(sub + 1) * P]
                        for part in range(3):
                            pe.wait_ge(rows_taken, START + 3 * (HG * TPB * v + hs) + part - 2)
                            if part < 2:
                                for c in range(3 * part, 3 * part + 3):
                                    mm = nc.tensor.matmul(ring[:, c, :], q, ks[:, h, chunks[c]], start=True, stop=True)
                            else:
                                nc.tensor.matmul(o_ps[:, 0:P], q, ks[:, h, chunks[6]], start=True, stop=True)
                                mm = nc.tensor.matmul(o_ps[:, P:P + TAIL], q, kt[:, h * SEL:h * SEL + TAIL],
                                                      start=True, stop=True)
                            mm.then_inc(rows_ready, 1)
                    pe.wait_ge(m_ready, v + 1)
                    for hs in range(HG * TPB):
                        h, sub = divmod(hs, TPB)
                        mm = nc.tensor.matmul(ring[0:1, h, sub * P:(sub + 1) * P], m_col[:, hs:hs + 1], ident[:, :],
                                              start=True, stop=True)
                    mm.then_inc(m_turned, 1)
                    pe.wait_ge(m_rows, v + 1)

                if exact:
                    with pe.Fori(0, NG) as g:
                        with pe.Fori(0, NB // 2) as half:
                            for par in range(2):
                                U = Unit(g + NG, half, par)
                                row_maxima(U, g * NB + U.b)
                                for n in range(RING):
                                    scores(U, n, True)
                                unit(U, None, lambda t: None)
                                denominators(U)
                    return

                sample(0)
                for n in range(RING):
                    scores(Unit(0, 0, 0), n, True)
                for g in groups(pe):
                    def first_side(t):
                        if t == AT_L:
                            if not isinstance(g, int):
                                denominators(Unit(g - 1, NB // 2 - 1, 1))
                        project(Task(g, 0), t)

                    def side_of(U, prev):
                        def side(t):
                            if t == AT_L:
                                pe.wait_ge(v_done, START + Task(g, U.b).t)
                                denominators(prev)
                            project(Task(g, U.b), t)
                        return side

                    def last_side(t):
                        if t == AT_L:
                            pe.wait_ge(v_done, START + KB * (g + 1))
                            denominators(Unit(g, NB // 2 - 1, 0))
                        if t == AT_SAMPLE:
                            sample(g + 1)

                    unit(Unit(g, 0, 0), Unit(g, 0, 1), first_side)
                    with pe.Fori(1, NB // 2) as half:
                        U = [Unit(g, half - 1, 0), Unit(g, half - 1, 1), Unit(g, half, 0), Unit(g, half, 1)]
                        unit(U[1], U[2], side_of(U[1], U[0]))
                        unit(U[2], U[3], side_of(U[2], U[1]))
                    unit(Unit(g, NB // 2 - 1, 1), Unit(g + 1, 0, 0), last_side)

                U = [Unit(LAST - 1, NB // 2 - 1, 1)] + [Unit(LAST, b // 2, b % 2) for b in range(NB)]
                for b in range(NB):
                    def side(t):
                        if t == AT_L:
                            if b >= 2:
                                pe.wait_ge(y_added, START + TPB * (b - 2) + 1)
                            if b == 0:
                                pe.wait_ge(sample_max, NG)
                            denominators(U[b])
                        for j, at in enumerate(AT_Y):
                            if b >= 2 and at <= t < at + NG:
                                if t == at:
                                    pe.wait_ge(l_taken, START + U[b + 1].u - (1 if j == 0 else 0))
                                    pe.wait_ge(y_added, START + TPB * (b - 2) + j)
                                output_step(b - 2, j, t - at, l_ps[:, :])
                    unit(U[b + 1], U[b + 2] if b + 1 < NB else None, side)
                denominators(U[NB])
                for b in (NB - 2, NB - 1):
                    for j in range(TPB):
                        i = TPB * (b - NB + 2) + j
                        if i >= 2 * RING:
                            pe.wait_ge(y_added, START + TPB * (NB - 2) + i - 2 * RING + 1)
                        for g in range(NG):
                            output_step(b, j, g, ring[:, i % (2 * RING), :])

            def act_run(act, first_G, exact):
                bias = zero_bias if exact else shift

                def take_o(U):
                    act.wait_ge(o_ready, START + U.u + 1)
                    act.wait_ge(o_out, START + 16 * U.u)
                    nc.scalar.activation(o_sb[:, :], o_ps[:, :], ACT.Copy).then_inc(o_taken, 1)

                def take_l(U):
                    act.wait_ge(l_ready, START + U.u + 1)
                    act.wait_ge(l_out, START + 16 * U.u)
                    nc.scalar.activation(l_sb[:, :], l_ps[:, :], ACT.Copy).then_inc(l_taken, 1)

                def unit(U, side):
                    for t in range(NT):
                        act.wait_ge(pv_done, START + NT * U.u + t - PR + 1)
                        if t < PR:
                            act.wait_ge(p_added, START + ADDS * (U.u - 1) + add_of(t + NT - PR))
                        else:
                            act.wait_ge(p_added, START + ADDS * U.u + add_of(t - PR))
                        for pair in range(2):
                            n = 2 * t + pair
                            act.wait_ge(s_ready, scores_done(U, n))
                            bank = 2 * (n % RING)
                            nc.scalar.activation(pt[t % PR][:, 2 * pair:2 * pair + 2, :], ring[:, bank:bank + 2, :],
                                                 ACT.Exp, scale=SCALE, bias=bias[:, :]).then_inc(e_done, 1)
                        side(t)
                    act.wait_ge(s_ready, scores_done(U, ITEMS - 1))
                    rows = TAIL * HG
                    nc.scalar.activation(pt_tail[U.par][:, :], ring[0:rows, 2 * ((ITEMS - 1) % RING), :],
                                         ACT.Exp, scale=SCALE, bias=bias[0:rows, :]).then_inc(e_done, 1)

                def new_shift(G):
                    if not (isinstance(G, int) and G == 0):
                        act.wait_ge(e_done, G * NB * ITEMS)
                    act.wait_ge(group_max, START + G + 1)
                    nc.scalar.activation(shift[:, :], g_max[:, :], ACT.Copy, scale=-SCALE).then_inc(shift_ready, 1)
                    act.wait_ge(shift_ready, G + 1)

                def split_hi(T):
                    act.wait_ge(kv_ready, START + 2 * T.t + 1)
                    act.wait_ge(k_out, START + 32 * T.t)
                    nc.scalar.activation(k_hi.bitcast(F32R), l_ps[:, :], ACT.Identity, bias=bk_c).then_inc(hi_done, 1)

                if exact:
                    with act.Fori(0, NG) as g:
                        with act.Fori(0, NB // 2) as half:
                            for par in range(2):
                                U = Unit(g + NG, half, par)
                                unit(U, lambda t: None)
                                take_o(U)
                                take_l(U)
                    return

                def side_of(prev, T):
                    def side(t):
                        if prev is not None and t == 0:
                            take_o(prev)
                        if prev is not None and t == AT_L + 2:
                            take_l(prev)
                        if T is not None and t == AT_K + FT:
                            split_hi(T)
                    return side

                new_shift(0)
                for g in groups(act):
                    before = None if isinstance(g, int) else Unit(g - 1, NB // 2 - 1, 1)
                    unit(Unit(g, 0, 0), side_of(before, Task(g, 0)))
                    with act.Fori(1, NB // 2) as half:
                        U = [Unit(g, half - 1, 0), Unit(g, half - 1, 1), Unit(g, half, 0)]
                        unit(U[1], side_of(U[0], Task(g, U[1].b)))
                        unit(U[2], side_of(U[1], Task(g, U[2].b)))
                    unit(Unit(g, NB // 2 - 1, 1), side_of(Unit(g, NB // 2 - 1, 0), None))
                    new_shift(g + 1)
                U = [Unit(LAST - 1, NB // 2 - 1, 1)] + [Unit(LAST, b // 2, b % 2) for b in range(NB)]
                for b in range(NB):
                    unit(U[b + 1], side_of(U[b], None))
                take_o(U[NB])
                take_l(U[NB])

            def dve_run(dve, first_G, exact):
                def unit(U, side):
                    for t in [1] + list(range(3, NT)):
                        k = add_of(t)
                        dve.wait_ge(e_done, scores_done(U, 2 * t + 1))
                        a = acc[U.par][(k - 1) % 2]
                        if k <= 2:
                            dve.wait_ge(l_ready, START + U.u - 1)
                        else:
                            dve.wait_ge(p_added, START + ADDS * U.u + k - 2)
                        nc.vector.tensor_tensor(a[:, :, :], (pt[t - 1] if k <= 2 else a)[:, :, :], pt[t % PR][:, :, :],
                                                ALU.add).then_inc(p_added, 1)
                        side(t)

                def take_sample(G):
                    dve.wait_ge(sample_ready, G + 1)
                    dve.wait_ge(group_max, START + G)
                    nc.vector.reduce_max(s_max[:, :], l_ps[:, :], AX_X).then_inc(sample_max, 1)

                def split_lo(T):
                    dve.wait_ge(hi_done, T.t + 1)
                    nc.vector.scalar_tensor_tensor(out=k_lo.bitcast(F32R), in0=l_ps[:, :], scalar=bk_c, in1=k_hi,
                                                   op0=ALU.add, op1=ALU.subtract).then_inc(lo_done, 1)

                def take_v(T):
                    dve.wait_ge(kv_ready, START + 2 * T.t + 2)
                    dve.wait_ge(v_out, START + 16 * T.t)
                    nc.vector.tensor_tensor(v_st, l_ps[:, :].rearrange("p (j n) -> p j n", j=TPB), bv_b,
                                            ALU.add).then_inc(v_done, 1)

                def take_reciprocals(b):
                    dve.wait_ge(l_blk_in, 16 * (b + 1))
                    if b > 0:
                        dve.wait_ge(r_blk_out, 16 * b)
                    nc.vector.reciprocal(r_blk[:, :], l_blk[:, :]).then_inc(r_blk_done, 1)

                def divide(b):
                    dve.wait_ge(or_in, 16 * (1 + HG) * (b + 1))
                    dve.wait_ge(y_done, TPB * b)
                    nc.vector.tensor_tensor(on, o_in, r_b, ALU.mult).then_inc(on_ready, 1)

                def add_y(b, j, bank):
                    dve.wait_ge(y_done, TPB * b + j + 1)
                    dve.wait_ge(xy_in[j // 2], 16 * (b + 1))
                    nc.vector.tensor_tensor(xy[:, j, :], bank, xy[:, j, :], ALU.add).then_inc(y_added, 1)

                def row_maxima(v):
                    for hs in range(HG * TPB):
                        for part in range(3):
                            dve.wait_ge(rows_ready, 3 * (HG * TPB * v + hs) + part + 1)
                            src = o_ps[:, 0:P + TAIL] if part == 2 else \
                                ring[:, 3 * part:3 * part + 3, :].rearrange("p b n -> p (b n)")
                            nc.vector.reduce_max(m_part[:, hs, part:part + 1], src, AX_X).then_inc(rows_taken, 1)
                    dve.wait_ge(rows_taken, START + 3 * HG * TPB * (v + 1))
                    nc.vector.tensor_reduce(m_col[:, :], m_part[:, :, :], op=ALU.max, axis=AX_X,
                                            negate=True).then_inc(m_ready, 1)
                    dve.wait_ge(m_turned, v + 1)
                    nc.vector.tensor_copy(m_row[0:1, :, :], ring[0:1, 0:HG, :]).then_inc(m_rows, 1)

                if exact:
                    with dve.Fori(0, NG) as g:
                        with dve.Fori(0, NB // 2) as half:
                            for par in range(2):
                                U = Unit(g + NG, half, par)
                                row_maxima(g * NB + U.b)
                                unit(U, lambda t: None)
                    return

                take_sample(0)
                for g in groups(dve):
                    def task_side(T):
                        def side(t):
                            if t == AT_K + FT + 1:
                                split_lo(T)
                            if t == AT_V + TPB:
                                take_v(T)
                        return side

                    unit(Unit(g, 0, 0), task_side(Task(g, 0)))
                    with dve.Fori(1, NB // 2) as half:
                        for U in (Unit(g, half - 1, 1), Unit(g, half, 0)):
                            unit(U, task_side(Task(g, U.b)))
                    unit(Unit(g, NB // 2 - 1, 1), lambda t: take_sample(g + 1) if t == AT_SAMPLE + 1 else None)
                for b in range(NB):
                    def side(t):
                        if b >= 2:
                            for j, at in enumerate(AT_Y):
                                if t == at + NG - 1:
                                    add_y(b - 2, j, l_ps[:, :])
                        if b >= 1:
                            if t == AT_L + 7:
                                take_reciprocals(b - 1)
                            if t == NT - 1:
                                divide(b - 1)
                    unit(Unit(LAST, b // 2, b % 2), side)
                for j in range(TPB):
                    add_y(NB - 2, j, ring[:, j, :])
                take_reciprocals(NB - 1)
                divide(NB - 1)
                for j in range(TPB):
                    add_y(NB - 1, j, ring[:, (TPB + j) % (2 * RING), :])

            def reciprocals(dve, runs):
                dve.wait_ge(l_in, 16 * runs)
                nc.vector.reciprocal(r_all, l_all).then_inc(r_ready, 1)

            def check_shift(dve):
                nc.vector.reduce_max(l_top[:, 0:1], l_all, AX_X).then_inc(l_step, 1)
                dve.wait_ge(r_ready, 1)
                nc.vector.reduce_max(l_top[:, 1:2], r_all, AX_X).then_inc(l_step, 1)
                dve.wait_ge(l_step, 2)
                nc.vector.tensor_scalar(l_ok[:, 0:1], l_top[:, 0:1], SHIFT_OK_SUM, None, ALU.is_lt)
                nc.vector.tensor_scalar(l_ok[:, 1:2], l_top[:, 1:2], SHIFT_OK_RECIP, None,
                                        ALU.is_lt).then_inc(l_step, 1)
                dve.wait_ge(l_step, 3)
                nc.vector.tensor_tensor(l_ok[:, 2:3], l_ok[:, 0:1], l_ok[:, 1:2], ALU.mult).then_inc(l_step, 1)
                dve.wait_ge(flag_sum, 1)
                nc.vector.tensor_scalar(flag[:, :], l_ps[0:1, 0:1], P - 0.5, None, ALU.is_lt).then_inc(flag_ready, 1)

            with nc.Block() as block:
                @block.sync
                def _(sp):
                    sp.wait_ge(consts, 3)
                    transfers(sp)
                    load_sums(sp, 1)
                    with again(sp):
                        exact_transfers(sp)
                        load_sums(sp, 2)
                        store_reciprocals(sp)

                @block.gpsimd
                def _(pool):
                    raise_to_start(pool, from_start)
                    nc.gpsimd.memset(kt[:, :].bitcast(F32), 0.0).then_inc(consts, 1)
                    nc.gpsimd.memset(vt[:, :], 0.0).then_inc(consts, 1)
                    nc.gpsimd.memset(ones_blk[:, :], 1.0).then_inc(consts, 1)
                    blk = ones_blk[:, :].rearrange("p (h d) -> p h d", h=HG)
                    pool.wait_ge(consts, 3)
                    nc.gpsimd.affine_select(out=blk, in_=blk, compare_op=ALU.is_ge, fill=0.0, base=0,
                                            pattern=[[-TAIL, HG], [0, DH]], channel_multiplier=1).then_inc(consts, 1)
                    pool.wait_ge(consts, 4)
                    nc.gpsimd.affine_select(out=blk, in_=blk, compare_op=ALU.is_ge, fill=0.0, base=TAIL - 1,
                                            pattern=[[TAIL, HG], [0, DH]], channel_multiplier=-1).then_inc(consts, 1)
                    sample_maxima(pool)
                    with again(pool):
                        nc.gpsimd.memset(row1, 1.0).then_inc(exact_consts, 1)
                        nc.gpsimd.memset(row_tail, 0.0).then_inc(exact_consts, 1)
                        nc.gpsimd.memset(ident, 0.0).then_inc(exact_consts, 1)
                        pool.wait_ge(exact_consts, 3)
                        for h in range(HG):
                            nc.gpsimd.memset(row_tail[:, h * SEL:h * SEL + TAIL], 1.0).then_inc(exact_consts, 1)
                        nc.gpsimd.affine_select(out=ident, in_=ident, compare_op=ALU.not_equal, fill=1.0,
                                                base=0, pattern=[[-1, P]], channel_multiplier=1
                                                ).then_inc(exact_consts, 1)

                @block.tensor
                def _(pe):
                    pe.wait_ge(consts, 5)
                    pe.wait_ge(fills, 2)
                    pe_run(pe, 0, False)
                    pe.wait_ge(l_step, 4)
                    pe.wait_ge(l_taken, START + UNITS)
                    nc.tensor.matmul(l_ps[0:1, 0:1], l_ok[:, 2:3], ones[:, 0:1], start=True, stop=True
                                     ).then_inc(flag_sum, 1)
                    with again(pe):
                        pe_run(pe, NG, True)

                @block.scalar
                def _(act):
                    act.wait_ge(fills, 2)
                    act_run(act, 0, False)
                    with again(act):
                        act_run(act, NG, True)

                @block.vector
                def _(dve):
                    nc.vector.memset(ones[:, :], 1.0).then_inc(fills, 1)
                    nc.vector.memset(zero_bias[:, :], 0.0).then_inc(fills, 1)
                    dve_run(dve, 0, False)
                    reciprocals(dve, 1)
                    check_shift(dve)
                    with again(dve):
                        dve_run(dve, NG, True)
                        reciprocals(dve, 2)

    def exact_epilogue():
        with ExitStack() as st:
            def sb(name, shape, dt=F32):
                return st.enter_context(nc.sbuf_tensor(name, shape, dt))

            def sem(name):
                return st.enter_context(nc.semaphore(name))

            wp = sb("wp_e", [P, NG, H])
            o_in = [sb(f"o_in_e{i}", [P, NG, QB]) for i in range(2)]
            r_b = [sb(f"r_b_e{i}", [P, NG, QB]) for i in range(2)]
            on = [sb(f"on_e{i}", [P, NG, QB]) for i in range(2)]
            xb = [sb(f"xb_e{i}", [P, TPB, H]) for i in range(2)]
            y = [sb(f"y_e{i}", [P, TPB, H]) for i in range(2)]
            bank = st.enter_context(nc.psum_tensor("bank_e", [P, 8, 512], F32))

            w_in = sem("w_in_e")
            in_all = [sem(f"in_all_e{i}") for i in range(2)]
            xb_in = [sem(f"xb_in_e{i}") for i in range(2)]
            on_ready = sem("on_ready_e")
            y_done = sem("y_done_e")
            y_ready = sem("y_ready_e")
            y_out = [sem(f"y_out_e{i}") for i in range(2)]
            from_start = [on_ready, y_done, y_ready] + y_out

            def blocks(eng):
                with eng.Fori(0, NB // 2) as i:
                    yield i, 0, 2 * i
                    yield i, 1, 2 * i + 1

            with nc.Block() as block:
                @block.gpsimd
                def _(pool):
                    raise_to_start(pool, from_start)

                @block.sync
                def _(sp):
                    with again(sp):
                        sp.dma_start(wp[:, :, :], Wp.rearrange("(g p) n -> p g n", p=P)).then_inc(w_in, 16)
                        for i, par, b in blocks(sp):
                            cols = ds(b * QB, QB)
                            sp.wait_ge(on_ready, START + b - 1)
                            sp.dma_start(o_in[par][:, :, :],
                                         o_dram[:, cols].rearrange("(g p) q -> p g q", p=P)).then_inc(in_all[par], 16)
                            for j in range(HG):
                                src = r_dram[:, cols].rearrange("(g j) q -> j g q", j=HG)[j:j + 1, :, :]
                                sp.dma_start(r_b[par][j * DH:(j + 1) * DH, :, :],
                                             src.broadcast_to([DH, NG, QB])).then_inc(in_all[par], 16)
                            sp.wait_ge(y_ready, START + TPB * (b - 1))
                            sp.dma_start(xb[par][:, :, :],
                                         xb_dram[cols, :].rearrange("(j p) f -> p j f", p=P)).then_inc(xb_in[par], 16)

                @block.scalar
                def _(act):
                    with again(act):
                        for i, par, b in blocks(act):
                            act.wait_ge(y_ready, START + TPB * (b + 1))
                            act.dma_start(out2[ds(b * QB, QB), :].rearrange("(j p) f -> p j f", p=P),
                                          y[par][:, :, :]).then_inc(y_out[par], 16)
                        for par in range(2):
                            act.wait_ge(y_out[par], START + 16 * NB // 2)

                @block.tensor
                def _(pe):
                    with again(pe):
                        pe.wait_ge(w_in, 16)
                        for i, par, b in blocks(pe):
                            pe.wait_ge(on_ready, START + b + 1)
                            for j in range(TPB):
                                bk = TPB * par + j
                                pe.wait_ge(y_ready, START + TPB * (b - 2) + j + 1)
                                for g in range(NG):
                                    mm = nc.tensor.matmul(bank[:, bk, :], on[par][:, g, j * P:(j + 1) * P],
                                                          wp[:, g, :], start=(g == 0), stop=(g == NG - 1))
                                mm.then_inc(y_done, 1)

                @block.vector
                def _(dve):
                    def divide(i, par, b):
                        dve.wait_ge(in_all[par], 16 * (1 + HG) * (i + 1))
                        dve.wait_ge(y_done, START + TPB * (b - 1))
                        nc.vector.tensor_tensor(on[par][:, :, :], o_in[par][:, :, :], r_b[par][:, :, :],
                                                ALU.mult).then_inc(on_ready, 1)

                    def add_residual(i, par, b):
                        dve.wait_ge(xb_in[par], 16 * (i + 1))
                        dve.wait_ge(y_out[par], START + 16 * i)
                        for j in range(TPB):
                            dve.wait_ge(y_done, START + TPB * b + j + 1)
                            nc.vector.tensor_tensor(y[par][:, j, :], bank[:, TPB * par + j, :], xb[par][:, j, :],
                                                    ALU.add).then_inc(y_ready, 1)

                    with again(dve):
                        divide(0, 0, 0)
                        with dve.Fori(0, NB // 2 - 1) as i:
                            divide(i, 1, 2 * i + 1)
                            add_residual(i, 0, 2 * i)
                            divide(i + 1, 0, 2 * i + 2)
                            add_residual(i, 1, 2 * i + 1)
                        divide(NB // 2 - 1, 1, NB - 1)
                        add_residual(NB // 2 - 1, 0, NB - 2)
                        add_residual(NB // 2 - 1, 1, NB - 1)

    with outer:
        prologue()
        attention_and_check()
        exact_epilogue()


_INS = ['x', 'ctx_1024', 'cond_1024', 'L0_xcond_Wq', 'L0_xcond_bq', 'L0_xcond_Wkv', 'L0_xcond_bkv', 'L0_xcond_Wp',
        'L0_xcond_bp', 'L0_xcond_Wss_q', 'L0_xcond_bss_q', 'L0_xcond_Wss_kv', 'L0_xcond_bss_kv']


def kernel(**inputs):
    import numpy as _np
    import concourse.bacc as _bacc
    from concourse import mybir as _mybir
    from concourse.bass_utils import run_bass_kernel_spmd as _run

    nc = _bacc.Bacc("TRN2", target_bir_lowering=False, num_devices=1)
    arrays, args = {}, []
    for name in _INS:
        a = _np.ascontiguousarray(inputs[name])
        arrays[f"in_{name}_dram"] = a
        args.append(nc.dram_tensor(f"in_{name}_dram", a.shape, _mybir.dt.from_np(a.dtype), kind="ExternalInput").ap())
    shape = tuple(inputs['x'].shape)
    args.append(nc.dram_tensor("out_dram", shape, _mybir.dt.float32, kind="ExternalOutput").ap())
    cross_attention(nc, *args)
    r = _run(nc, [arrays], core_ids=[0])
    return r.results[0]["out_dram"]
```

```python
from contextlib import ExitStack

import concourse.bass as bass
from concourse import mybir

P = 128
F32 = mybir.dt.float32
F32R = mybir.dt.float32r
I32 = mybir.dt.int32
ALU = mybir.AluOpType
ACT = mybir.ActivationFunctionType
AX_X = mybir.AxisListType.X
RMAX = bass.bass_isa.ReduceOp.max
ds = bass.ds

EPS = 1e-5
NH = 16
SHIFT_OK_SUM = 1e25
SHIFT_OK_RECIP = 1e20


def cross_attention(nc, x, ctx, cond, Wq, bq, Wkv, bkv, Wp, bp, Wss_q, bss_q, Wss_kv, bss_kv, out):
    _, LQ, H = x.shape
    LKV = ctx.shape[1]
    DH = H // NH
    FT = H // P
    HG = P // DH
    NG = NH // HG
    QB = 512
    NB = LQ // QB
    TPB = QB // P
    NT = LKV // P
    TAIL = LKV - NT * P
    CT = 5
    NC = NT // CT
    KB = -(-LKV // QB)
    KP = KB * QB
    RING = 3
    PR = 5
    ADDS = NT - 1
    LAST = NG - 1
    ITEMS = 2 * NT + 1
    UNITS = NG * NB
    SCALE = float(DH) ** -0.5
    SEL = P + TAIL
    assert DH == 32 and HG == 4 and TAIL * HG <= 32 and ITEMS % RING == 0 and NT % PR == 0 and NT % CT == 0
    assert LKV - (KB - 1) * QB == P + TAIL and NB % 2 == 0 and KB == NB - 1

    x2, ctx2, out2 = x[0], ctx[0], out[0]
    q_dram = nc.dram_tensor("q_split", [2, H, LQ], F32).ap()
    k_dram = nc.dram_tensor("k_split", [2, H, KP], F32).ap()
    v_dram = nc.dram_tensor("v_full", [KP, H], F32).ap()
    xt_dram = nc.dram_tensor("ctx_t", [H, KP], F32).ap()
    xb_dram = nc.dram_tensor("x_bias", [LQ, H], F32).ap()
    o_dram = nc.dram_tensor("o_sums", [H, LQ], F32).ap()
    l_dram = nc.dram_tensor("l_sums", [NH, LQ], F32).ap()
    r_dram = nc.dram_tensor("l_recip", [NH, LQ], F32).ap()

    START = 64

    def raise_to_start(eng, sems):
        for s in sems:
            eng.sem_inc(s, START)

    outer = ExitStack()
    flag = outer.enter_context(nc.sbuf_tensor("flag", [1, 1], I32))
    flag_ready = outer.enter_context(nc.semaphore("flag_ready"))

    def again(eng):
        eng.wait_ge(flag_ready, 1)
        return eng.If(eng.value_load(flag[0:1, 0:1], min_val=0, max_val=1))

    def prologue():
        with ExitStack() as st:
            def sb(name, shape, dt=F32):
                return st.enter_context(nc.sbuf_tensor(name, shape, dt))

            def sem(name):
                return st.enter_context(nc.semaphore(name))

            ident = sb("ident", [P, P])
            one1 = sb("one1", [1, 1])
            cond_c = sb("cond_c", [P, FT])
            silu_e = sb("silu_e", [P, FT])
            silu_d = sb("silu_d", [P, FT])
            silu_r = sb("silu_r", [P, FT])
            silu_c = sb("silu_c", [P, FT])
            wss = [sb(f"wss{i}", [P, FT, 2 * H]) for i in range(2)]
            bss = sb("bss", [1, 2, 2 * H])
            ss_row = sb("ss_row", [1, 2, 2 * H])
            mod = sb("mod", [P, 2, 2 * FT])
            wq = sb("wq", [P, FT, H])
            wk0 = sb("wk0", [P, FT, P])
            wv0 = sb("wv0", [P, FT, P])
            bq_c = sb("bq_c", [P, FT])
            bk_c = sb("bk_c", [P, FT])
            bv0_b = sb("bv0_b", [P, TPB, P])
            bp_b = sb("bp_b", [P, H])
            xin = [sb(f"xin{i}", [P, TPB, H]) for i in range(2)]
            hn = [sb(f"hn{i}", [P, TPB, H]) for i in range(2)]
            xt = [sb(f"xt{i}", [P, FT, QB]) for i in range(2)]
            hi = [sb(f"hi{i}", [P, FT, QB], F32R) for i in range(2)]
            lo = [sb(f"lo{i}", [P, FT, QB], F32R) for i in range(2)]
            vs = sb("vs", [P, TPB, P])
            xb = sb("xb", [P, TPB, H])
            stats = sb("stats", [P, TPB, 6])
            aggr = sb("aggr", [P, TPB, 2])
            var_eps = sb("var_eps", [P, TPB])
            minus_half = sb("minus_half", [P, TPB])
            rstd = sb("rstd", [P, TPB])
            bank = st.enter_context(nc.psum_tensor("bank", [P, 8, 512], F32))

            consts = sem("consts")
            cond_in = sem("cond_in")
            wss_part_in = [[sem(f"wss_in{w}{half}") for half in range(2)] for w in range(2)]
            bss_in = sem("bss_in")
            bp_in = sem("bp_in")
            weights_in = sem("weights_in")
            silu_step = sem("silu_step")
            ss_done = sem("ss_done")
            ss_rows = sem("ss_rows")
            ss_cols = sem("ss_cols")
            mod_ready = sem("mod_ready")
            first_in = [sem(f"first_in{i}") for i in range(2)]
            x_in = [sem(f"x_in{i}") for i in range(2)]
            hi_ready = sem("hi_ready")
            rstd_ready = sem("rstd_ready")
            xb_ready = sem("xb_ready")
            wait_carrier = sem("wait_carrier")
            sp_carrier = sem("sp_carrier_p")
            stat_step = sem("stat_step")
            h_ready = sem("h_ready")
            t_ready = sem("t_ready")
            xt_ready = sem("xt_ready")
            proj_done = sem("proj_done")
            lo_ready = sem("lo_ready")
            v_ready = sem("v_ready")
            xb_out = sem("xb_out")
            xt_out = [sem(f"xt_out{i}") for i in range(2)]
            split_out = [sem(f"split_out{i}") for i in range(2)]
            v_out = sem("v_out")
            from_start = [stat_step, h_ready, t_ready, xt_ready, proj_done, lo_ready, v_ready, v_out, xb_out]
            from_start += split_out + xt_out

            class Blk:
                def __init__(self, half, off, kv, last=False):
                    self.half, self.off, self.kv, self.last = half, off, kv, last
                    self.n = 2 * half + off
                    self.par = off % 2
                    self.use = half + off // 2
                    self.splits = NB * FT + (self.n - NB) if kv else self.n * FT
                    self.results = NB * FT + 2 * (self.n - NB) if kv else self.n * FT
                    self.m_tiles = 1 if kv else FT

                def token0(self):
                    return (self.n - NB) * QB if self.kv else self.n * QB

            N_ALL = NB + KB

            def ahead(b, d):
                if isinstance(b.half, int):
                    n = b.n + d
                    return Blk(n // 2, n % 2, n >= NB, n == N_ALL - 1) if n < N_ALL else None
                return Blk(b.half, b.off + d, b.kv)

            def blocks(eng):
                with eng.Fori(0, NB // 2 - 1) as i:
                    yield Blk(i, 0, False)
                    yield Blk(i, 1, False)
                yield Blk(NB // 2 - 1, 0, False)
                yield Blk(NB // 2 - 1, 1, False)
                with eng.Fori(NB // 2, (N_ALL - 3) // 2) as i:
                    yield Blk(i, 0, True)
                    yield Blk(i, 1, True)
                for n in range(N_ALL - 3, N_ALL):
                    yield Blk(n // 2, n % 2, True, n == N_ALL - 1)

            with nc.Block() as block:
                @block.sync
                def _(sp):
                    def first_load(b):
                        sp.dma_start(xin[b][:, :, :], x2[b * QB:(b + 1) * QB, :].rearrange("(j p) f -> p j f", p=P)
                                     ).then_inc(first_in[b], 16)

                    sp.dma_start(cond_c[:, :], cond[0].rearrange("(t p) -> p t", p=P),
                                 allow_slow_non_contiguous=True).then_inc(cond_in, 16)
                    for w, bias in enumerate((bss_q, bss_kv)):
                        sp.dma_start(bss[:, w, :], bias.rearrange("(a n) -> a n", a=1)).then_inc(bss_in, 16)
                    for w, weight in enumerate((Wss_q, Wss_kv)):
                        for k in range(0, FT, 2):
                            rows = weight[k * P:(k + 2) * P, :].rearrange("(t p) n -> p t n", p=P)
                            sp.dma_start(wss[w][:, k:k + 2, :], rows).then_inc(wss_part_in[w][k // 2], 16)
                        if w == 0:
                            sp.dma_start(bp_b[:, :], bp.rearrange("(a n) -> a n", a=1)
                                         .broadcast_to([P, H])).then_inc(bp_in, 16)
                        first_load(w)
                    for b in blocks(sp):
                        cols = ds(b.token0(), QB)
                        if b.kv:
                            sp.wait_ge(xt_ready, START + FT * (b.n + 1))
                            sp.dma_start(xt_dram[:, cols].rearrange("(t p) q -> p t q", p=P),
                                         xt[b.par][:, :, :]).then_inc(xt_out[b.par], 16)
                        dst = (k_dram if b.kv else q_dram)[:, 0:b.m_tiles * P, :]
                        sp.wait_ge(lo_ready, START + b.splits + b.m_tiles)
                        sp.sem_inc(sp_carrier, 1)
                        for part, tile in ((0, hi), (1, lo)):
                            sp.dma_start(dst[part, :, cols].rearrange("(t p) q -> p t q", p=P),
                                         tile[b.par][:, 0:b.m_tiles, :].bitcast(F32)).then_inc(split_out[b.par], 16)
                        if b.kv:
                            sp.wait_ge(v_ready, START + b.n - NB + 1)
                            sp.dma_start(v_dram[cols, 0:P].rearrange("(j p) f -> p j f", p=P),
                                         vs[:, :, :]).then_inc(v_out, 16)
                    for par in range(2):
                        sp.wait_ge(split_out[par], START + 32 * ((N_ALL + 1 - par) // 2))
                        sp.wait_ge(xt_out[par], START + 16 * ((KB + 1 - par) // 2))
                    sp.wait_ge(v_out, START + 16 * KB)
                    sp.wait_ge(xb_out, START + 16 * NB)

                @block.gpsimd
                def _(pool):
                    raise_to_start(pool, from_start)
                    nc.gpsimd.memset(ident[:, :], 0.0).then_inc(consts, 1)
                    nc.gpsimd.memset(one1[:, :], 1.0).then_inc(consts, 1)
                    nc.gpsimd.memset(minus_half[:, :], -0.5).then_inc(consts, 1)
                    pool.wait_ge(consts, 3)
                    nc.gpsimd.affine_select(out=ident[:, :], in_=ident[:, :], compare_op=ALU.not_equal, fill=1.0,
                                            base=0, pattern=[[-1, P]], channel_multiplier=1).then_inc(consts, 1)

                    def inverse_deviation(b):
                        pool.wait_ge(stat_step, START + 3 * (b.n + 1))
                        nc.gpsimd.tensor_tensor(rstd[:, :], var_eps[:, :], minus_half[:, :],
                                                ALU.pow).then_inc(rstd_ready, 1)

                    def load(b):
                        pool.wait_ge(h_ready, START + b.n - 1)
                        src = ctx2 if b.kv else x2
                        full = 1 if b.last else TPB
                        pool.dma_start(xin[b.par][:, 0:full, :],
                                     src[ds(b.token0(), P * full), :].rearrange("(j p) f -> p j f", p=P)
                                     ).then_inc(x_in[b.par], 16)
                        if b.last:
                            pool.dma_start(xin[b.par][0:TAIL, full, :], ctx2[NT * P:LKV, :]).then_inc(x_in[b.par], 16)

                    inverse_deviation(Blk(0, 0, False))
                    for first, end, kv in ((1, NB // 2, False), (NB // 2, N_ALL // 2, True)):
                        with pool.Fori(first, end) as half:
                            load(Blk(half, 0, kv))
                            inverse_deviation(Blk(half - 1, 1, kv))
                            load(Blk(half, 1, kv))
                            inverse_deviation(Blk(half, 0, kv))
                    load(Blk(N_ALL // 2, 0, True, True))
                    inverse_deviation(Blk(N_ALL // 2 - 1, 1, True))
                    inverse_deviation(Blk(N_ALL // 2, 0, True, True))

                @block.tensor
                def _(pe):
                    pe.wait_ge(silu_step, 4)
                    for w in range(2):
                        for k in range(FT):
                            if k % 2 == 0:
                                pe.wait_ge(wss_part_in[w][k // 2], 16)
                            for half in range(2):
                                mm = nc.tensor.matmul(bank[0:1, 2 * w + half, :], silu_c[:, k:k + 1],
                                                      wss[w][:, k, half * H:(half + 1) * H],
                                                      start=(k == 0), stop=(k == FT - 1))
                        mm.then_inc(ss_done, 1)
                    pe.wait_ge(consts, 4)
                    for w in range(2):
                        pe.wait_ge(ss_rows, w + 1)
                        for c in range(2 * FT):
                            col = 2 * FT * w + c
                            mm = nc.tensor.matmul(bank[:, 4, col:col + 1], ss_row[0:1, w, c * P:(c + 1) * P],
                                                  one1[0:1, 0:1], start=True, stop=True)
                    mm.then_inc(ss_cols, 1)

                    def transposes(b):
                        pe.wait_ge(h_ready, START + b.n + 1)
                        for f in range(FT):
                            pe.wait_ge(xt_ready, START + FT * (b.n - 1) + f + 1)
                            for j in range(TPB):
                                mm = nc.tensor.transpose(bank[:, f, j * P:(j + 1) * P],
                                                         hn[b.par][:, j, f * P:(f + 1) * P], ident[:, :])
                            mm.then_inc(t_ready, 1)

                    transposes(Blk(0, 0, False))
                    pe.wait_ge(weights_in, 16 * (5 + TPB))
                    for b in blocks(pe):
                        if ahead(b, 1):
                            transposes(ahead(b, 1))
                        pe.wait_ge(xt_ready, START + FT * (b.n + 1))
                        if not b.kv:
                            for m in range(FT):
                                pe.wait_ge(lo_ready, START + FT * (b.n - 1) + m + 1)
                                for k in range(FT):
                                    mm = nc.tensor.matmul(bank[:, 4 + m, :], wq[:, k, m * P:(m + 1) * P],
                                                          xt[b.par][:, k, :], start=(k == 0), stop=(k == FT - 1))
                                mm.then_inc(proj_done, 1)
                        else:
                            pe.wait_ge(lo_ready, START + b.splits - 1)
                            pe.wait_ge(v_ready, START + b.n - NB - 1)
                            for k in range(FT):
                                mm = nc.tensor.matmul(bank[:, 4 + 2 * b.par, :], wk0[:, k, :], xt[b.par][:, k, :],
                                                      start=(k == 0), stop=(k == FT - 1))
                            mm.then_inc(proj_done, 1)
                            for j in range(TPB):
                                for k in range(FT):
                                    mm = nc.tensor.matmul(bank[:, 5 + 2 * b.par, j * P:(j + 1) * P],
                                                          xt[b.par][:, k, j * P:(j + 1) * P], wv0[:, k, :],
                                                          start=(k == 0), stop=(k == FT - 1))
                            mm.then_inc(proj_done, 1)

                @block.scalar
                def _(act):
                    act.wait_ge(cond_in, 16)
                    nc.scalar.activation(silu_e[:, :], cond_c[:, :], ACT.Exp, scale=-1.0).then_inc(silu_step, 1)
                    act.wait_ge(wss_part_in[0][1], 16)
                    act.dma_start(wq[:, :, :], Wq.rearrange("(t p) n -> p t n", p=P)).then_inc(weights_in, 16)
                    act.dma_start(bq_c[:, :], bq.rearrange("(t p) -> p t", p=P),
                                  allow_slow_non_contiguous=True).then_inc(weights_in, 16)
                    for w, col in ((wk0, 0), (wv0, H)):
                        act.dma_start(w[:, :, :],
                                      Wkv[:, col:col + P].rearrange("(t p) n -> p t n", p=P)).then_inc(weights_in, 16)
                    act.dma_start(bk_c[:, :], bkv[0:H].rearrange("(t p) -> p t", p=P),
                                  allow_slow_non_contiguous=True).then_inc(weights_in, 16)
                    for j in range(TPB):
                        act.dma_start(bv0_b[:, j, :], bkv[H:H + P].rearrange("(a n) -> a n", a=1)
                                      .broadcast_to([P, P])).then_inc(weights_in, 16)
                    def modulate(b):
                        first_kv = isinstance(b.n, int) and b.n == NB
                        act.wait_ge(proj_done, START + b.results - (2 if b.kv and not first_kv else FT))
                        if b.kv:
                            act.wait_ge(xt_out[b.par], START + 16 * (b.use - NB // 2))
                        w = 1 if b.kv else 0
                        for f in range(FT):
                            act.wait_ge(t_ready, START + FT * b.n + f + 1)
                            nc.scalar.activation(xt[b.par][:, f, :], bank[:, f, :], ACT.Identity,
                                                 scale=mod[:, w, f:f + 1],
                                                 bias=mod[:, w, FT + f:FT + f + 1]).then_inc(xt_ready, 1)

                    def store_residual(b):
                        act.wait_ge(xb_ready, b.n + 1)
                        act.dma_start(xb_dram[ds(b.token0(), QB), :].rearrange("(j p) f -> p j f", p=P),
                                     xb[:, :, :]).then_inc(xb_out, 16)

                    store_residual(Blk(0, 0, False))
                    act.wait_ge(mod_ready, 1)
                    act.wait_ge(weights_in, 16 * (5 + TPB))
                    modulate(Blk(0, 0, False))
                    for b in blocks(act):
                        if ahead(b, 1):
                            modulate(ahead(b, 1))
                            if not ahead(b, 1).kv:
                                store_residual(ahead(b, 1))
                        bias = bk_c if b.kv else bq_c
                        act.wait_ge(split_out[b.par], START + 32 * b.use)
                        for m in range(b.m_tiles):
                            act.wait_ge(proj_done, START + b.results + m + 1)
                            src = bank[:, 4 + (2 * b.par if b.kv else m), :]
                            nc.scalar.activation(hi[b.par][:, m, :], src, ACT.Identity,
                                                 bias=bias[:, m:m + 1]).then_inc(hi_ready, 1)

                @block.vector
                def _(dve):
                    dve.wait_ge(silu_step, 1)
                    nc.vector.tensor_scalar_add(silu_d[:, :], silu_e[:, :], 1.0).then_inc(silu_step, 1)
                    dve.wait_ge(silu_step, 2)
                    nc.vector.reciprocal(silu_r[:, :], silu_d[:, :]).then_inc(silu_step, 1)
                    dve.wait_ge(silu_step, 3)
                    nc.vector.tensor_tensor(silu_c[:, :], silu_r[:, :], cond_c[:, :], ALU.mult).then_inc(silu_step, 1)

                    tiles = range(TPB)

                    def statistics(b):
                        if isinstance(b.n, int) and b.n < 2:
                            dve.wait_ge(first_in[b.n], 16)
                        else:
                            dve.wait_ge(x_in[b.par], 16 * b.use + (16 if b.last else 0))
                        for j in tiles:
                            i = nc.vector.bn_stats(stats[:, j, :], xin[b.par][:, j, :])
                        i.then_inc(stat_step, 1)
                        dve.wait_ge(stat_step, START + 3 * b.n + 1)
                        dve.sem_inc(wait_carrier, 1)
                        for j in tiles:
                            i = nc.vector.bn_aggr(aggr[:, j, :], stats[:, j, :])
                        i.then_inc(stat_step, 1)
                        dve.wait_ge(stat_step, START + 3 * b.n + 2)
                        nc.vector.tensor_scalar_add(var_eps[:, :], aggr[:, :, 1], EPS).then_inc(stat_step, 1)

                    def scale(b):
                        if not b.kv:
                            dve.wait_ge(xb_out, START + 16 * b.n)
                            for j in tiles:
                                i = nc.vector.tensor_tensor(xb[:, j, :], xin[b.par][:, j, :], bp_b[:, :], ALU.add)
                            i.then_inc(xb_ready, 1)
                        dve.wait_ge(t_ready, START + FT * (b.n - 1))
                        dve.wait_ge(rstd_ready, b.n + 1)
                        for j in tiles:
                            i = nc.vector.tensor_scalar(hn[b.par][:, j, :], xin[b.par][:, j, :], aggr[:, j, 0:1],
                                                        rstd[:, j:j + 1], ALU.subtract, ALU.mult)
                        i.then_inc(h_ready, 1)

                    def normalise(b):
                        statistics(b)
                        scale(b)

                    dve.wait_ge(bp_in, 16)
                    normalise(Blk(0, 0, False))
                    for w in range(2):
                        if w == 1:
                            statistics(Blk(0, 1, False))
                        dve.wait_ge(ss_done, w + 1)
                        dve.wait_ge(bss_in, 32)
                        nc.vector.tensor_tensor(ss_row[0:1, w, :],
                                                bank[0:1, 2 * w:2 * w + 2, :].rearrange("p a n -> p (a n)"),
                                                bss[0:1, w, :], ALU.add).then_inc(ss_rows, 1)
                    dve.wait_ge(weights_in, 16 * (5 + TPB))
                    dve.wait_ge(ss_cols, 1)
                    cols = bank[:, 4, 0:4 * FT].rearrange("p (w c) -> p w c", w=2)
                    nc.vector.tensor_scalar_add(mod[:, :, 0:FT], cols[:, :, 0:FT], 1.0)
                    nc.vector.tensor_copy(mod[:, :, FT:2 * FT], cols[:, :, FT:2 * FT]).then_inc(mod_ready, 1)
                    scale(Blk(0, 1, False))

                    for b in blocks(dve):
                        if ahead(b, 2):
                            normalise(ahead(b, 2))
                        bias = bk_c if b.kv else bq_c
                        for m in range(b.m_tiles):
                            dve.wait_ge(hi_ready, b.splits + m + 1)
                            src = bank[:, 4 + (2 * b.par if b.kv else m), :]
                            nc.vector.scalar_tensor_tensor(out=lo[b.par][:, m, :], in0=src, scalar=bias[:, m:m + 1],
                                                           in1=hi[b.par][:, m, :].bitcast(F32),
                                                           op0=ALU.add, op1=ALU.subtract).then_inc(lo_ready, 1)
                        if b.kv:
                            dve.wait_ge(v_out, START + 16 * (b.n - NB))
                            dve.wait_ge(proj_done, START + b.results + 2)
                            nc.vector.tensor_tensor(vs[:, :, :].rearrange("p j f -> p (j f)"), bank[:, 5 + 2 * b.par, :],
                                                    bv0_b[:, :, :].rearrange("p j f -> p (j f)"),
                                                    ALU.add).then_inc(v_ready, 1)

    def attention_and_check():
        with ExitStack() as st:
            def sb(name, shape, dt=F32):
                return st.enter_context(nc.sbuf_tensor(name, shape, dt))

            def sem(name):
                return st.enter_context(nc.semaphore(name))

            ks = sb("ks", [P, HG, NT * P], F32R)
            kt = sb("kt", [P, HG * SEL], F32R)
            vg = sb("vg", [P, NT, P])
            vt = sb("vt", [TAIL * HG, P])
            qs = [sb(f"qs{i}", [P, HG, QB], F32R) for i in range(2)]
            pt = [sb(f"pt{i}", [P, HG, QB]) for i in range(PR)]
            pt_tail = [sb(f"pt_tail{i}", [TAIL * HG, QB]) for i in range(2)]
            acc = [sb(f"acc{i}", [P, HG, QB]) for i in range(2)]
            acc2 = sb("acc2", [P, HG, QB])
            o_sb = sb("o_sb", [P, QB])
            l_sb = sb("l_sb", [P, QB])
            ones = sb("ones", [P, DH])
            ones_blk = sb("ones_blk", [TAIL * HG, P])
            zero_bias = sb("zero_bias", [P, 1])
            s_max = sb("s_max", [P, 1])
            g_max = sb("g_max", [P, 1])
            shift = sb("shift", [P, 1])
            l_blk = sb("l_blk", [P, NH * QB // P])
            r_blk = sb("r_blk", [P, NH * QB // P])
            l_top = sb("l_top", [P, 2])
            l_ok = sb("l_ok", [P, 3])

            W5 = H * 4
            work = sb("work", [P, 5 * W5])
            xt = work[:, 0:W5].rearrange("p (t q) -> p t q", t=FT)
            wk = work[:, W5:W5 + H].rearrange("p (t n) -> p t n", t=FT)
            wv = work[:, W5 + H:W5 + 2 * H].rearrange("p (t n) -> p t n", t=FT)
            bk_c = work[:, 2 * W5 - 1:2 * W5]
            bv_b = work[:, W5 + 2 * H:W5 + 3 * H].rearrange("p (j n) -> p j n", j=TPB)
            k_hi = work[:, 2 * W5:2 * W5 + H]
            k_lo = work[:, 2 * W5 + H:2 * W5 + 2 * H]
            v_st = work[:, 2 * W5 + 2 * H:2 * W5 + 3 * H].rearrange("p (j n) -> p j n", j=TPB)

            def quarter(i):
                return work[:, i * W5:(i + 1) * W5].rearrange("p (g q) -> p g q", g=NG)

            wp, o_in, r_b, on, xy = (quarter(i) for i in range(5))
            l_all = sb("l_all", [P, NH * LQ // P])[:, :]
            r_all = sb("r_all", [P, NH * LQ // P])[:, :]
            m_row = work[0:1, 0:W5].rearrange("p (h q) -> p h q", h=HG)
            row_tail = work[0:1, W5:W5 + HG * SEL]
            row1 = work[0:1, 2 * W5:2 * W5 + P]
            ident = work[:, 3 * W5:3 * W5 + P]
            m_part = work[:, 4 * W5:4 * W5 + 3 * HG * TPB].rearrange("p (c k) -> p c k", k=3)
            m_col = work[:, 4 * W5 + H:4 * W5 + H + HG * TPB]
            ring = st.enter_context(nc.psum_tensor("ring", [P, 2 * RING, 512], F32))
            o_ps = st.enter_context(nc.psum_tensor("o_ps", [P, 512], F32))
            l_ps = st.enter_context(nc.psum_tensor("l_ps", [P, 512], F32))

            consts = sem("consts_a")
            fills = sem("fills")
            exact_consts = sem("exact_consts")
            k_in = [sem(f"k_in{c}") for c in range(NC)]
            tail_in = sem("tail_in")
            q_in = [sem(f"q_in{i}") for i in range(2)]
            s_ready = sem("s_ready")
            e_done = sem("e_done")
            sample_ready = sem("sample_ready")
            sample_max = sem("sample_max")
            wait_carrier = sem("wait_carrier_a")
            sp_carrier = sem("sp_carrier")
            shift_ready = sem("shift_ready")
            task_w_in = sem("task_w_in")
            xt_in = sem("xt_in")
            hi_done = sem("hi_done")
            rows_ready = sem("rows_ready")
            m_ready = sem("m_ready")
            m_turned = sem("m_turned")
            m_rows = sem("m_rows")
            wp_in = sem("wp_in")
            l_blk_in = sem("l_blk_in")
            r_blk_done = sem("r_blk_done")
            r_blk_out = sem("r_blk_out")
            or_in = sem("or_in")
            xy_in = [sem(f"xy_in{i}") for i in range(2)]
            y_done = sem("y_done")
            l_step = sem("l_step")
            l_in = sem("l_in")
            r_last = sem("r_last")
            r_out = sem("r_out")
            r_ready = sem("r_ready")
            flag_sum = sem("flag_sum")
            pv_done = sem("pv_done")
            p_added = sem("p_added")
            o_ready = sem("o_ready")
            o_taken = sem("o_taken")
            l_ready = sem("l_ready")
            l_taken = sem("l_taken")
            group_max = sem("group_max")
            rows_taken = sem("rows_taken")
            o_out = sem("o_out")
            l_out = sem("l_out")
            kv_ready = sem("kv_ready")
            lo_done = sem("lo_done")
            v_done = sem("v_done")
            k_out = sem("k_out")
            v_out = sem("v_out_a")
            on_ready = sem("on_ready")
            y_added = sem("y_added")
            y_out = [sem(f"y_out{i}") for i in range(2)]
            from_start = [pv_done, p_added, o_ready, o_taken, l_ready, l_taken, group_max, rows_taken, o_out, l_out,
                          kv_ready, lo_done, v_done, k_out, v_out, on_ready, y_added] + y_out

            AT_L = 4
            AT_K = 7
            V_STEPS = (18, 18, 18, 19, 19, 19, 20, 20, 21, 21, 22, 22, 23, 23, 24, 24)
            AT_Y = (0, 9, 14, 19)
            AT_SAMPLE = 18

            class Unit:
                def __init__(self, G, half, par):
                    self.G, self.par = G, par
                    self.b = 2 * half + par
                    self.u = G * NB + self.b
                    self.use = G * (NB // 2) + half
                    self.starts_group = isinstance(half, int) and half == 0 and par == 0

            def groups(eng):
                yield 0
                with eng.Fori(1, LAST) as g:
                    yield g

            def scores_done(U, n):
                return U.u * ITEMS + n + 1

            def add_of(t):
                return max(t - 1, 1) if t < 2 or t > 3 else 2

            def tail_of(t, h):
                return t[:, h * P:(h + 1) * P]

            def load_q(sp, g, U):
                sp.wait_ge(o_ready, START + U.u - 1)
                for r in range(4):
                    src = q_dram[r % 2, ds(g * P, P), ds(U.b * QB, QB)].rearrange("(h d) q -> d h q", d=DH)
                    sp.dma_start(qs[U.par][r * DH:(r + 1) * DH, :, :].bitcast(F32), src).then_inc(q_in[U.par], 16)

            def load_keys(sp, g, G, parts=range(NC)):
                for c in parts:
                    sp.wait_ge(pv_done, START + (G * NB - 1) * NT + CT * (c + 1))
                    keys = slice(c * CT * P, (c + 1) * CT * P)
                    for r in range(4):
                        src = k_dram[r // 2, ds(g * P, P), keys].rearrange("(h d) k -> d h k", d=DH)
                        sp.dma_start(ks[r * DH:(r + 1) * DH, :, keys].bitcast(F32), src).then_inc(k_in[c], 16)
                    sp.dma_start(vg[:, c * CT:(c + 1) * CT, :],
                                 v_dram[keys, ds(g * P, P)].rearrange("(t p) n -> p t n", p=P)).then_inc(k_in[c], 16)

            def load_tail(sp, g, G):
                sp.wait_ge(o_ready, START + G * NB)
                for r in range(4):
                    src = k_dram[r // 2, ds(g * P, P), NT * P:LKV].rearrange("(h d) k -> d h k", d=DH)
                    dst = kt[r * DH:(r + 1) * DH, :].rearrange("p (h c) -> p h c", c=SEL)[:, :, 0:TAIL]
                    sp.dma_start(dst.bitcast(F32), src).then_inc(tail_in, 16)
                for h in range(HG):
                    sp.dma_start(vt[TAIL * h:TAIL * (h + 1), h * DH:(h + 1) * DH],
                                 v_dram[NT * P:LKV, ds(g * P + h * DH, DH)]).then_inc(tail_in, 16)

            def store_o(sp, g, U):
                sp.wait_ge(o_taken, START + U.u + 1)
                sp.dma_start(o_dram[ds(g * P, P), ds(U.b * QB, QB)], o_sb[:, :]).then_inc(o_out, 16)

            def store_l(sp, g, U):
                sp.wait_ge(l_taken, START + U.u + 1)
                sp.dma_start(l_dram[ds(g * HG, HG), ds(U.b * QB, QB)], l_sb[0:P:DH, :]).then_inc(l_out, 16)

            def load_task_weights(sp, g):
                sp.wait_ge(v_done, START + KB * g)
                for w, col in ((wk, 0), (wv, H)):
                    sp.dma_start(w, Wkv[:, ds((g + 1) * P + col, P)].rearrange("(t p) n -> p t n", p=P)
                                 ).then_inc(task_w_in, 16)
                sp.dma_start(bk_c, bkv[ds((g + 1) * P, P)].rearrange("(p a) -> p a", a=1)).then_inc(task_w_in, 16)
                for j in range(TPB):
                    sp.dma_start(bv_b[:, j, :], bkv[ds((g + 1) * P + H, P)].rearrange("(a n) -> a n", a=1)
                                 .broadcast_to([P, P])).then_inc(task_w_in, 16)

            TASK_W = 16 * (3 + TPB)

            class Task:
                def __init__(self, g, b):
                    self.g, self.b = g, b
                    self.t = g * KB + b

            def load_xt(sp, T):
                sp.wait_ge(kv_ready, START + 2 * T.t)
                sp.sem_inc(sp_carrier, 1)
                sp.dma_start(xt, xt_dram[:, ds(T.b * QB, QB)].rearrange("(t p) q -> p t q", p=P)).then_inc(xt_in, 16)

            def store_k(sp, T):
                cols = ds(T.b * QB, QB)
                rows = ds((T.g + 1) * P, P)
                sp.wait_ge(lo_done, START + T.t + 1)
                sp.dma_start(k_dram[0, rows, cols], k_hi).then_inc(k_out, 16)
                sp.dma_start(k_dram[1, rows, cols], k_lo).then_inc(k_out, 16)

            def store_v(sp, T):
                cols = ds(T.b * QB, QB)
                rows = ds((T.g + 1) * P, P)
                sp.wait_ge(v_done, START + T.t + 1)
                sp.dma_start(v_dram[cols, rows].rearrange("(j p) f -> p j f", p=P), v_st).then_inc(v_out, 16)

            def load_xy(sp, b, half):
                sp.wait_ge(y_out[half], START + 16 * b)
                sp.dma_start(xy[:, 2 * half:2 * half + 2, :],
                             xb_dram[ds(b * QB + 2 * half * P, 2 * P), :].rearrange("(j p) f -> p j f", p=P)
                             ).then_inc(xy_in[half], 16)

            def store_y(sp, b, half):
                sp.wait_ge(y_added, START + TPB * b + 2 * half + 2)
                sp.dma_start(out2[ds(b * QB + 2 * half * P, 2 * P), :].rearrange("(j p) f -> p j f", p=P),
                             xy[:, 2 * half:2 * half + 2, :]).then_inc(y_out[half], 16)

            def invert(sp, b, groups):
                cols, heads = ds(b * QB, QB), groups * HG
                rows = heads * P // NH
                sp.wait_ge(l_out, START + 16 * (LAST * NB + b + (1 if groups == NG else 0)))
                sp.dma_start(l_blk[0:rows, :], l_dram[0:heads, cols].rearrange("h (a q) -> h a q", a=P // NH)
                             ).then_inc(l_blk_in, 16)
                sp.wait_ge(r_blk_done, b + 1)
                sp.dma_start(r_dram[0:heads, cols].rearrange("h (a q) -> h a q", a=P // NH), r_blk[0:rows, :]
                             ).then_inc(r_blk_out, 16)

            def fetch(sp, b, groups):
                cols = ds(b * QB, QB)
                sp.wait_ge(o_out, START + 16 * (LAST * NB + b + (1 if groups == NG else 0)))
                sp.wait_ge(on_ready, START + b)
                sp.dma_start(o_in[:, 0:groups, :], o_dram[0:groups * P, cols].rearrange("(g p) q -> p g q", p=P)
                             ).then_inc(or_in, 16)
                sp.wait_ge(r_blk_out, 16 * (b + 1))
                for j in range(HG):
                    src = r_dram[0:groups * HG, cols].rearrange("(g j) q -> j g q", j=HG)[j:j + 1, :, :]
                    sp.dma_start(r_b[j * DH:(j + 1) * DH, 0:groups, :], src.broadcast_to([DH, groups, QB])
                                 ).then_inc(or_in, 16)

            def transfers(sp):
                load_q(sp, 0, Unit(0, 0, 0))
                load_keys(sp, 0, 0, [0])
                for g in groups(sp):
                    load_task_weights(sp, g)
                    load_xt(sp, Task(g, 0))
                    if isinstance(g, int):
                        load_keys(sp, 0, 0, range(1, NC))
                        sp.wait_ge(consts, 3)
                    load_tail(sp, g, g)
                    load_q(sp, g, Unit(g, 0, 1))
                    if not isinstance(g, int):
                        store_o(sp, g - 1, Unit(g - 1, NB // 2 - 1, 1))
                        store_l(sp, g - 1, Unit(g - 1, NB // 2 - 1, 1))
                    store_k(sp, Task(g, 0))

                    def unit(U, prev, nxt):
                        load_q(sp, g, nxt)
                        load_xt(sp, Task(g, U.b))
                        store_o(sp, g, prev)
                        store_v(sp, Task(g, prev.b))
                        store_l(sp, g, prev)
                        store_k(sp, Task(g, U.b))

                    with sp.Fori(1, NB // 2) as half:
                        unit(Unit(g, half - 1, 1), Unit(g, half - 1, 0), Unit(g, half, 0))
                        unit(Unit(g, half, 0), Unit(g, half - 1, 1), Unit(g, half, 1))
                    load_q(sp, g + 1, Unit(g + 1, 0, 0))
                    store_o(sp, g, Unit(g, NB // 2 - 1, 0))
                    store_v(sp, Task(g, KB - 1))
                    store_l(sp, g, Unit(g, NB // 2 - 1, 0))
                    sp.wait_ge(k_out, START + 32 * KB * (g + 1))
                    sp.wait_ge(v_out, START + 16 * KB * (g + 1))
                    load_keys(sp, g + 1, g + 1)

                U = [Unit(LAST, b // 2, b % 2) for b in range(NB)]
                load_tail(sp, LAST, LAST)
                load_q(sp, LAST, U[1])
                store_o(sp, LAST - 1, Unit(LAST - 1, NB // 2 - 1, 1))
                store_l(sp, LAST - 1, Unit(LAST - 1, NB // 2 - 1, 1))
                sp.dma_start(wp, Wp.rearrange("(g p) n -> p g n", p=P)).then_inc(wp_in, 16)
                load_q(sp, LAST, U[2])
                store_o(sp, LAST, U[0])
                store_l(sp, LAST, U[0])
                invert(sp, 0, NG)
                fetch(sp, 0, NG)
                load_xy(sp, 0, 0)
                for b in range(2, NB):
                    if b + 1 < NB:
                        load_q(sp, LAST, U[b + 1])
                    load_xy(sp, b - 2, 1)
                    store_o(sp, LAST, U[b - 1])
                    store_l(sp, LAST, U[b - 1])
                    invert(sp, b - 1, NG)
                    fetch(sp, b - 1, NG)
                    store_y(sp, b - 2, 0)
                    load_xy(sp, b - 1, 0)
                    if b == NB - 1:
                        invert(sp, b, LAST)
                    store_y(sp, b - 2, 1)
                load_xy(sp, NB - 2, 1)
                fetch(sp, NB - 1, LAST)
                store_o(sp, LAST, U[NB - 1])
                store_l(sp, LAST, U[NB - 1])
                for b in (NB - 2, NB - 1):
                    store_y(sp, b, 0)
                    if b + 1 < NB:
                        load_xy(sp, b + 1, 0)
                    store_y(sp, b, 1)
                    if b + 1 < NB:
                        load_xy(sp, b + 1, 1)
                sp.wait_ge(o_out, START + 16 * UNITS)
                for half in range(2):
                    sp.wait_ge(y_out[half], START + 16 * NB)

            def exact_transfers(sp):
                with sp.Fori(0, NG) as g:
                    G = g + NG
                    load_q(sp, g, Unit(G, 0, 0))
                    load_keys(sp, g, G)
                    load_tail(sp, g, G)
                    load_q(sp, g, Unit(G, 0, 1))
                    store_o(sp, g, Unit(G, 0, 0))
                    store_l(sp, g, Unit(G, 0, 0))
                    with sp.Fori(1, NB // 2) as half:
                        load_q(sp, g, Unit(G, half, 0))
                        store_o(sp, g, Unit(G, half - 1, 1))
                        store_l(sp, g, Unit(G, half - 1, 1))
                        load_q(sp, g, Unit(G, half, 1))
                        store_o(sp, g, Unit(G, half, 0))
                        store_l(sp, g, Unit(G, half, 0))
                    store_o(sp, g, Unit(G, NB // 2 - 1, 1))
                    store_l(sp, g, Unit(G, NB // 2 - 1, 1))

            def load_sums(queue, runs):
                queue.wait_ge(l_out, START + 16 * runs * UNITS)
                queue.dma_start(l_all, l_dram.rearrange("h (a q) -> (h a) q", a=P // NH)).then_inc(l_in, 16)

            def store_reciprocals(sp):
                sp.wait_ge(r_ready, 2)
                sp.dma_start(r_dram.rearrange("h (a q) -> (h a) q", a=P // NH), r_all).then_inc(r_out, 16)
                sp.wait_ge(r_out, 16)

            def sample_maxima(pool):
                with pool.Fori(0, NG) as G:
                    pool.wait_ge(sample_max, G + 1)
                    pool.sem_inc(wait_carrier, 1)
                    nc.gpsimd.partition_all_reduce(g_max[:, :], s_max[:, :], P, RMAX).then_inc(group_max, 1)

            def pe_run(pe, exact):
                def scores(U, n, first):
                    bank = 2 * (n % RING)
                    if n >= RING:
                        pe.wait_ge(e_done, scores_done(U, n - RING))
                    elif not first:
                        pe.wait_ge(e_done, U.u * ITEMS + n - RING + 1)
                        if n == 0 and U.starts_group:
                            pe.wait_ge(k_in[0], 80 * (U.G + 1))
                    if n == 0:
                        pe.wait_ge(q_in[U.par], 64 * (U.use + 1))
                    if n == ITEMS - 1:
                        if U.starts_group and not exact:
                            pe.wait_ge(tail_in, 128 * (U.G + 1))
                        for h in range(HG):
                            mm = nc.tensor.matmul(ring[:, bank, :], tail_of(kt, h), qs[U.par][:, h, :],
                                                  start=(h == 0), stop=(h == HG - 1 and not exact))
                        if exact:
                            for h in range(HG):
                                mm = nc.tensor.matmul(ring[:, bank, :], tail_of(row_tail, h), m_row[0:1, h, :],
                                                      start=False, stop=(h == HG - 1))
                    else:
                        t, pair = divmod(n, 2)
                        if U.starts_group and not exact and pair == 0 and t % CT == 0 and t > 0:
                            pe.wait_ge(k_in[t // CT], 80 * (U.G + 1))
                        for i in range(2):
                            h = 2 * pair + i
                            mm = nc.tensor.matmul(ring[:, bank + i, :], ks[:, h, t * P:(t + 1) * P],
                                                  qs[U.par][:, h, :], start=True, stop=not exact)
                            if exact:
                                mm = nc.tensor.matmul(ring[:, bank + i, :], row1[0:1, :], m_row[0:1, h, :],
                                                      start=False, stop=True)
                    mm.then_inc(s_ready, 1)

                def weigh(U, t):
                    pe.wait_ge(e_done, scores_done(U, 2 * t + 1))
                    if t == 0:
                        pe.wait_ge(o_taken, START + U.u)
                    for h in range(HG):
                        cols = slice(h * DH, (h + 1) * DH)
                        mm = nc.tensor.matmul(o_ps[cols, :], vg[:, t, cols], pt[t % PR][:, h, :],
                                              start=(t == 0), stop=False, skip_group_check=True)
                    mm.then_inc(pv_done, 1)

                def weigh_tail(U):
                    pe.wait_ge(e_done, scores_done(U, ITEMS - 1))
                    nc.tensor.matmul(o_ps[:, :], vt[:, :], pt_tail[U.par][:, :], start=False, stop=True,
                                     skip_group_check=True).then_inc(o_ready, 1)

                def denominators(U, steps=(0, 1)):
                    for step in steps:
                        if step == 0:
                            pe.wait_ge(l_taken, START + U.u)
                            pe.wait_ge(p_added, START + ADDS * (U.u + 1))
                            for h in range(HG):
                                nc.tensor.matmul(l_ps[h * DH:(h + 1) * DH, :], ones[:, :], acc[U.par][:, h, :],
                                                 start=True, stop=False, skip_group_check=True)
                        else:
                            nc.tensor.matmul(l_ps[:, :], ones_blk[:, :], pt_tail[U.par][:, :], start=False, stop=True,
                                             skip_group_check=True).then_inc(l_ready, 1)

                def unit(U, nxt, side):
                    for t in range(NT):
                        for n in (2 * t + RING, 2 * t + RING + 1):
                            if n < ITEMS:
                                scores(U, n, exact)
                            elif nxt is not None:
                                scores(nxt, n - ITEMS, False)
                        weigh(U, t)
                        if t == NT - 1:
                            weigh_tail(U)
                        side(t)
                    if nxt is not None:
                        scores(nxt, RING - 1, False)

                def sample(G):
                    pe.wait_ge(q_in[0], 64 * (Unit(G, 0, 0).use + 1))
                    pe.wait_ge(k_in[0], 80 * (G + 1))
                    pe.wait_ge(l_taken, START + Unit(G, 0, 0).u - 1)
                    for h in range(HG):
                        mm = nc.tensor.matmul(l_ps[:, h * P:(h + 1) * P], ks[:, h, 0:P], qs[0][:, h, 0:P],
                                              start=True, stop=True)
                    mm.then_inc(sample_ready, 1)

                def project(T, t):
                    half, k = divmod(t - AT_K, FT)
                    if t == AT_K:
                        pe.wait_ge(task_w_in, TASK_W * (T.g + 1))
                        pe.wait_ge(xt_in, 16 * (T.t + 1))
                        pe.wait_ge(l_taken, START + T.g * NB + T.b)
                    if half in (0, 1):
                        cols = slice(half * QB // 2, (half + 1) * QB // 2)
                        mm = nc.tensor.matmul(l_ps[:, cols], wk[:, k, :], xt[:, k, cols],
                                              start=(k == 0), stop=(k == FT - 1))
                        if k == FT - 1 and half == 1:
                            mm.then_inc(kv_ready, 1)
                    if t == V_STEPS[0]:
                        pe.wait_ge(lo_done, START + T.t + 1)
                    for i, at in enumerate(V_STEPS):
                        if at == t:
                            j, k = divmod(i, FT)
                            mm = nc.tensor.matmul(l_ps[:, j * P:(j + 1) * P], xt[:, k, j * P:(j + 1) * P], wv[:, k, :],
                                                  start=(k == 0), stop=(k == FT - 1))
                            if i == FT * TPB - 1:
                                mm.then_inc(kv_ready, 1)

                def output_step(b, j, g, bank):
                    if g == 0:
                        if b == 0 and j == 0:
                            pe.wait_ge(wp_in, 16)
                        pe.wait_ge(on_ready, START + b + 1)
                    divided = o_in if b == NB - 1 else on
                    mm = nc.tensor.matmul(bank, divided[:, g, j * P:(j + 1) * P], wp[:, g, :],
                                          start=(g == 0), stop=(g == NG - 1))
                    if g == NG - 1:
                        mm.then_inc(y_done, 1)

                def row_maxima(U, v):
                    pe.wait_ge(q_in[U.par], 64 * (U.use + 1))
                    for c in range(NC):
                        pe.wait_ge(k_in[c], 80 * (U.G + 1))
                    pe.wait_ge(tail_in, 128 * (U.G + 1))
                    pe.wait_ge(o_taken, START + U.u)
                    pe.wait_ge(exact_consts, 4 + HG)
                    chunks = [slice(c * 512, min((c + 1) * 512, NT * P)) for c in range((NT * P + 511) // 512)]
                    for hs in range(HG * TPB):
                        h, sub = divmod(hs, TPB)
                        q = qs[U.par][:, h, sub * P:(sub + 1) * P]
                        for part in range(3):
                            pe.wait_ge(rows_taken, START + 3 * (HG * TPB * v + hs) + part - 2)
                            if part < 2:
                                for c in range(3 * part, 3 * part + 3):
                                    mm = nc.tensor.matmul(ring[:, c, :], q, ks[:, h, chunks[c]], start=True, stop=True)
                            else:
                                nc.tensor.matmul(o_ps[:, 0:P], q, ks[:, h, chunks[6]], start=True, stop=True)
                                mm = nc.tensor.matmul(o_ps[:, P:P + TAIL], q, kt[:, h * SEL:h * SEL + TAIL],
                                                      start=True, stop=True)
                            mm.then_inc(rows_ready, 1)
                    pe.wait_ge(m_ready, v + 1)
                    for hs in range(HG * TPB):
                        h, sub = divmod(hs, TPB)
                        mm = nc.tensor.matmul(ring[0:1, h, sub * P:(sub + 1) * P], m_col[:, hs:hs + 1], ident[:, :],
                                              start=True, stop=True)
                    mm.then_inc(m_turned, 1)
                    pe.wait_ge(m_rows, v + 1)

                if exact:
                    with pe.Fori(0, NG) as g:
                        with pe.Fori(0, NB // 2) as half:
                            for par in range(2):
                                U = Unit(g + NG, half, par)
                                row_maxima(U, g * NB + U.b)
                                for n in range(RING):
                                    scores(U, n, True)
                                unit(U, None, lambda t: None)
                                denominators(U)
                    return

                sample(0)
                for n in range(RING):
                    scores(Unit(0, 0, 0), n, True)
                for g in groups(pe):
                    def first_side(t):
                        if 0 <= t - AT_L < 2 and not isinstance(g, int):
                            denominators(Unit(g - 1, NB // 2 - 1, 1), [t - AT_L])
                        project(Task(g, 0), t)

                    def side_of(U, prev):
                        def side(t):
                            if t == AT_L:
                                pe.wait_ge(v_done, START + Task(g, U.b).t)
                            if 0 <= t - AT_L < 2:
                                denominators(prev, [t - AT_L])
                            project(Task(g, U.b), t)
                        return side

                    def last_side(t):
                        if t == AT_L:
                            pe.wait_ge(v_done, START + KB * (g + 1))
                        if 0 <= t - AT_L < 2:
                            denominators(Unit(g, NB // 2 - 1, 0), [t - AT_L])
                        if t == AT_SAMPLE:
                            sample(g + 1)

                    unit(Unit(g, 0, 0), Unit(g, 0, 1), first_side)
                    with pe.Fori(1, NB // 2) as half:
                        U = [Unit(g, half - 1, 0), Unit(g, half - 1, 1), Unit(g, half, 0), Unit(g, half, 1)]
                        unit(U[1], U[2], side_of(U[1], U[0]))
                        unit(U[2], U[3], side_of(U[2], U[1]))
                    unit(Unit(g, NB // 2 - 1, 1), Unit(g + 1, 0, 0), last_side)

                U = [Unit(LAST - 1, NB // 2 - 1, 1)] + [Unit(LAST, b // 2, b % 2) for b in range(NB)]
                for b in range(NB):
                    def side(t):
                        if t == AT_L + 1:
                            if b >= 2:
                                pe.wait_ge(y_added, START + TPB * (b - 2) + 1)
                            if b == 0:
                                pe.wait_ge(sample_max, NG)
                        if 0 <= t - AT_L - 1 < 2:
                            denominators(U[b], [t - AT_L - 1])
                        for j, at in enumerate(AT_Y):
                            if b >= 2 and at <= t < at + NG:
                                if t == at:
                                    pe.wait_ge(l_taken, START + U[b + 1].u - (1 if j == 0 else 0))
                                    pe.wait_ge(y_added, START + TPB * (b - 2) + j)
                                output_step(b - 2, j, t - at, l_ps[:, :])
                    unit(U[b + 1], U[b + 2] if b + 1 < NB else None, side)
                for b in (NB - 2, NB - 1):
                    for j in range(TPB):
                        if b == NB - 2 and j == 2:
                            denominators(U[NB])
                        i = TPB * (b - NB + 2) + j
                        if i >= 2 * RING:
                            pe.wait_ge(y_added, START + TPB * (NB - 2) + i - 2 * RING + 1)
                        for g in range(NG):
                            output_step(b, j, g, ring[:, i % (2 * RING), :])

            def act_run(act, exact):
                bias = zero_bias if exact else shift

                def take_o(U):
                    act.wait_ge(o_ready, START + U.u + 1)
                    act.wait_ge(o_out, START + 16 * U.u)
                    nc.scalar.activation(o_sb[:, :], o_ps[:, :], ACT.Copy).then_inc(o_taken, 1)

                def take_l(U):
                    act.wait_ge(l_ready, START + U.u + 1)
                    act.wait_ge(l_out, START + 16 * U.u)
                    nc.scalar.activation(l_sb[:, :], l_ps[:, :], ACT.Copy).then_inc(l_taken, 1)

                def unit(U, side):
                    for t in range(NT):
                        act.wait_ge(pv_done, START + NT * U.u + t - PR + 1)
                        if t < PR:
                            act.wait_ge(p_added, START + ADDS * (U.u - 1) + add_of(t + NT - PR))
                        else:
                            act.wait_ge(p_added, START + ADDS * U.u + add_of(t - PR))
                        for pair in range(2):
                            n = 2 * t + pair
                            act.wait_ge(s_ready, scores_done(U, n))
                            bank = 2 * (n % RING)
                            nc.scalar.activation(pt[t % PR][:, 2 * pair:2 * pair + 2, :], ring[:, bank:bank + 2, :],
                                                 ACT.Exp, scale=SCALE, bias=bias[:, :]).then_inc(e_done, 1)
                        side(t)
                    act.wait_ge(s_ready, scores_done(U, ITEMS - 1))
                    rows = TAIL * HG
                    nc.scalar.activation(pt_tail[U.par][:, :], ring[0:rows, 2 * ((ITEMS - 1) % RING), :],
                                         ACT.Exp, scale=SCALE, bias=bias[0:rows, :]).then_inc(e_done, 1)

                def new_shift(G):
                    if not (isinstance(G, int) and G == 0):
                        act.wait_ge(e_done, G * NB * ITEMS)
                    act.wait_ge(group_max, START + G + 1)
                    nc.scalar.activation(shift[:, :], g_max[:, :], ACT.Copy, scale=-SCALE).then_inc(shift_ready, 1)
                    act.wait_ge(shift_ready, G + 1)

                def split_hi(T):
                    act.wait_ge(kv_ready, START + 2 * T.t + 1)
                    act.wait_ge(k_out, START + 32 * T.t)
                    nc.scalar.activation(k_hi.bitcast(F32R), l_ps[:, :], ACT.Identity, bias=bk_c).then_inc(hi_done, 1)

                if exact:
                    with act.Fori(0, NG) as g:
                        with act.Fori(0, NB // 2) as half:
                            for par in range(2):
                                U = Unit(g + NG, half, par)
                                unit(U, lambda t: None)
                                take_o(U)
                                take_l(U)
                    return

                def side_of(prev, T, at_l=AT_L + 3):
                    def side(t):
                        if prev is not None and t == 0:
                            take_o(prev)
                        if prev is not None and t == at_l:
                            take_l(prev)
                        if T is not None and t == AT_K + 2 * FT + 1:
                            split_hi(T)
                    return side

                new_shift(0)
                for g in groups(act):
                    before = None if isinstance(g, int) else Unit(g - 1, NB // 2 - 1, 1)
                    unit(Unit(g, 0, 0), side_of(before, Task(g, 0)))
                    with act.Fori(1, NB // 2) as half:
                        U = [Unit(g, half - 1, 0), Unit(g, half - 1, 1), Unit(g, half, 0)]
                        unit(U[1], side_of(U[0], Task(g, U[1].b)))
                        unit(U[2], side_of(U[1], Task(g, U[2].b)))
                    unit(Unit(g, NB // 2 - 1, 1), side_of(Unit(g, NB // 2 - 1, 0), None))
                    new_shift(g + 1)
                U = [Unit(LAST - 1, NB // 2 - 1, 1)] + [Unit(LAST, b // 2, b % 2) for b in range(NB)]
                for b in range(NB):
                    unit(U[b + 1], side_of(U[b], None, AT_L + 4))
                take_o(U[NB])
                take_l(U[NB])
                load_sums(act, 1)

            def dve_run(dve, exact):
                def unit(U, side):
                    sums = (acc[U.par], acc2)
                    for t in [1] + list(range(3, NT)):
                        k = add_of(t)
                        dve.wait_ge(e_done, scores_done(U, 2 * t + 1))
                        if k == 1:
                            dve.wait_ge(l_ready, START + U.u - 1)
                        elif k == 2:
                            dve.wait_ge(p_added, START + ADDS * U.u)
                        else:
                            dve.wait_ge(p_added, START + ADDS * U.u + k - 2)
                        a = sums[(k - 1) % 2]
                        nc.vector.tensor_tensor(a[:, :, :], (pt[t - 1] if k <= 2 else a)[:, :, :], pt[t % PR][:, :, :],
                                                ALU.add).then_inc(p_added, 1)
                        side(t)
                    dve.wait_ge(p_added, START + ADDS * U.u + ADDS - 1)
                    nc.vector.tensor_tensor(sums[0][:, :, :], sums[0][:, :, :], acc2[:, :, :],
                                            ALU.add).then_inc(p_added, 1)

                def take_sample(G):
                    dve.wait_ge(sample_ready, G + 1)
                    dve.wait_ge(group_max, START + G)
                    nc.vector.reduce_max(s_max[:, :], l_ps[:, :], AX_X).then_inc(sample_max, 1)

                def split_lo(T):
                    dve.wait_ge(hi_done, T.t + 1)
                    nc.vector.scalar_tensor_tensor(out=k_lo.bitcast(F32R), in0=l_ps[:, :], scalar=bk_c, in1=k_hi,
                                                   op0=ALU.add, op1=ALU.subtract).then_inc(lo_done, 1)

                def take_v(T):
                    dve.wait_ge(kv_ready, START + 2 * T.t + 2)
                    dve.wait_ge(v_out, START + 16 * T.t)
                    nc.vector.tensor_tensor(v_st, l_ps[:, :].rearrange("p (j n) -> p j n", j=TPB), bv_b,
                                            ALU.add).then_inc(v_done, 1)

                def take_reciprocals(b):
                    dve.wait_ge(l_blk_in, 16 * (b + 1))
                    if b > 0:
                        dve.wait_ge(r_blk_out, 16 * b)
                    nc.vector.reciprocal(r_blk[:, :], l_blk[:, :]).then_inc(r_blk_done, 1)

                def divide(b):
                    dve.wait_ge(or_in, 16 * (1 + HG) * (b + 1))
                    dve.wait_ge(y_done, TPB * b)
                    nc.vector.tensor_tensor(on, o_in, r_b, ALU.mult).then_inc(on_ready, 1)

                def divide_last():
                    dve.wait_ge(or_in, 16 * (1 + HG) * NB)
                    nc.vector.tensor_tensor(o_in[:, 0:LAST, :], o_in[:, 0:LAST, :], r_b[:, 0:LAST, :], ALU.mult)
                    dve.wait_ge(l_taken, START + UNITS)
                    nc.vector.reciprocal(r_b[:, LAST, :], l_sb[:, :]).then_inc(r_last, 1)
                    dve.wait_ge(r_last, 1)
                    nc.vector.tensor_tensor(o_in[:, LAST, :], o_sb[:, :], r_b[:, LAST, :], ALU.mult
                                            ).then_inc(on_ready, 1)

                def add_y(b, j, bank):
                    dve.wait_ge(y_done, TPB * b + j + 1)
                    dve.wait_ge(xy_in[j // 2], 16 * (b + 1))
                    nc.vector.tensor_tensor(xy[:, j, :], bank, xy[:, j, :], ALU.add).then_inc(y_added, 1)

                def row_maxima(v):
                    for hs in range(HG * TPB):
                        for part in range(3):
                            dve.wait_ge(rows_ready, 3 * (HG * TPB * v + hs) + part + 1)
                            src = o_ps[:, 0:P + TAIL] if part == 2 else \
                                ring[:, 3 * part:3 * part + 3, :].rearrange("p b n -> p (b n)")
                            nc.vector.reduce_max(m_part[:, hs, part:part + 1], src, AX_X).then_inc(rows_taken, 1)
                    dve.wait_ge(rows_taken, START + 3 * HG * TPB * (v + 1))
                    nc.vector.tensor_reduce(m_col[:, :], m_part[:, :, :], op=ALU.max, axis=AX_X,
                                            negate=True).then_inc(m_ready, 1)
                    dve.wait_ge(m_turned, v + 1)
                    nc.vector.tensor_copy(m_row[0:1, :, :], ring[0:1, 0:HG, :]).then_inc(m_rows, 1)

                if exact:
                    with dve.Fori(0, NG) as g:
                        with dve.Fori(0, NB // 2) as half:
                            for par in range(2):
                                U = Unit(g + NG, half, par)
                                row_maxima(g * NB + U.b)
                                unit(U, lambda t: None)
                    return

                take_sample(0)
                for g in groups(dve):
                    def task_side(T, before):
                        def side(t):
                            if before is not None and t == 1:
                                take_v(before)
                            if T is not None and t == AT_K + 2 * FT + 1:
                                split_lo(T)
                            if T is None and t == AT_SAMPLE + 1:
                                take_sample(g + 1)
                        return side

                    unit(Unit(g, 0, 0), task_side(Task(g, 0), None))
                    with dve.Fori(1, NB // 2) as half:
                        U = [Unit(g, half - 1, 0), Unit(g, half - 1, 1), Unit(g, half, 0)]
                        for before, now in ((U[0], U[1]), (U[1], U[2])):
                            unit(now, task_side(Task(g, now.b), Task(g, before.b)))
                    unit(Unit(g, NB // 2 - 1, 1), task_side(None, Task(g, KB - 1)))
                for b in range(NB):
                    def side(t):
                        if b >= 2:
                            for j, at in enumerate(AT_Y):
                                if t == at + NG - 1:
                                    add_y(b - 2, j, l_ps[:, :])
                        if b >= 1:
                            if t == AT_L + 10:
                                take_reciprocals(b - 1)
                            if t == NT - 3 and b == NB - 1:
                                take_reciprocals(b)
                            if t == NT - 2:
                                divide(b - 1)
                    unit(Unit(LAST, b // 2, b % 2), side)
                divide_last()
                for j in range(TPB):
                    add_y(NB - 2, j, ring[:, j, :])
                reciprocals(dve, 1)
                test_range(dve)
                for j in range(TPB):
                    add_y(NB - 1, j, ring[:, (TPB + j) % (2 * RING), :])

            def reciprocals(dve, runs):
                dve.wait_ge(l_in, 16 * runs)
                nc.vector.reciprocal(r_all, l_all).then_inc(r_ready, 1)

            def test_range(dve):
                nc.vector.reduce_max(l_top[:, 0:1], l_all, AX_X).then_inc(l_step, 1)
                dve.wait_ge(r_ready, 1)
                nc.vector.reduce_max(l_top[:, 1:2], r_all, AX_X).then_inc(l_step, 1)
                dve.wait_ge(l_step, 2)
                nc.vector.tensor_scalar(l_ok[:, 0:1], l_top[:, 0:1], SHIFT_OK_SUM, None, ALU.is_lt)
                nc.vector.tensor_scalar(l_ok[:, 1:2], l_top[:, 1:2], SHIFT_OK_RECIP, None,
                                        ALU.is_lt).then_inc(l_step, 1)
                dve.wait_ge(l_step, 3)
                nc.vector.tensor_tensor(l_ok[:, 2:3], l_ok[:, 0:1], l_ok[:, 1:2], ALU.mult).then_inc(l_step, 1)

            def decide(dve):
                dve.wait_ge(flag_sum, 1)
                nc.vector.tensor_scalar(flag[:, :], l_ps[0:1, 0:1], P - 0.5, None, ALU.is_lt).then_inc(flag_ready, 1)

            with nc.Block() as block:
                @block.sync
                def _(sp):
                    transfers(sp)
                    with again(sp):
                        exact_transfers(sp)
                        sp.wait_ge(o_out, START + 16 * 2 * UNITS)
                        load_sums(sp, 2)
                        store_reciprocals(sp)

                @block.gpsimd
                def _(pool):
                    raise_to_start(pool, from_start)
                    nc.gpsimd.memset(kt[:, :].bitcast(F32), 0.0).then_inc(consts, 1)
                    nc.gpsimd.memset(vt[:, :], 0.0).then_inc(consts, 1)
                    nc.gpsimd.memset(ones_blk[:, :], 1.0).then_inc(consts, 1)
                    blk = ones_blk[:, :].rearrange("p (h d) -> p h d", h=HG)
                    pool.wait_ge(consts, 3)
                    nc.gpsimd.affine_select(out=blk, in_=blk, compare_op=ALU.is_ge, fill=0.0, base=0,
                                            pattern=[[-TAIL, HG], [0, DH]], channel_multiplier=1).then_inc(consts, 1)
                    pool.wait_ge(consts, 4)
                    nc.gpsimd.affine_select(out=blk, in_=blk, compare_op=ALU.is_ge, fill=0.0, base=TAIL - 1,
                                            pattern=[[TAIL, HG], [0, DH]], channel_multiplier=-1).then_inc(consts, 1)
                    sample_maxima(pool)
                    with again(pool):
                        nc.gpsimd.memset(row1, 1.0).then_inc(exact_consts, 1)
                        nc.gpsimd.memset(row_tail, 0.0).then_inc(exact_consts, 1)
                        nc.gpsimd.memset(ident, 0.0).then_inc(exact_consts, 1)
                        pool.wait_ge(exact_consts, 3)
                        for h in range(HG):
                            nc.gpsimd.memset(row_tail[:, h * SEL:h * SEL + TAIL], 1.0).then_inc(exact_consts, 1)
                        nc.gpsimd.affine_select(out=ident, in_=ident, compare_op=ALU.not_equal, fill=1.0,
                                                base=0, pattern=[[-1, P]], channel_multiplier=1
                                                ).then_inc(exact_consts, 1)

                @block.tensor
                def _(pe):
                    pe.wait_ge(consts, 5)
                    pe.wait_ge(fills, 2)
                    pe_run(pe, False)
                    pe.wait_ge(l_step, 4)
                    pe.wait_ge(l_taken, START + UNITS)
                    nc.tensor.matmul(l_ps[0:1, 0:1], l_ok[:, 2:3], ones[:, 0:1], start=True, stop=True
                                     ).then_inc(flag_sum, 1)
                    with again(pe):
                        pe_run(pe, True)

                @block.scalar
                def _(act):
                    act.wait_ge(fills, 2)
                    act_run(act, False)
                    with again(act):
                        act_run(act, True)

                @block.vector
                def _(dve):
                    nc.vector.memset(ones[:, :], 1.0).then_inc(fills, 1)
                    nc.vector.memset(zero_bias[:, :], 0.0).then_inc(fills, 1)
                    dve_run(dve, False)
                    decide(dve)
                    with again(dve):
                        dve_run(dve, True)
                        reciprocals(dve, 2)

    def exact_epilogue():
        with ExitStack() as st:
            def sb(name, shape, dt=F32):
                return st.enter_context(nc.sbuf_tensor(name, shape, dt))

            def sem(name):
                return st.enter_context(nc.semaphore(name))

            wp = sb("wp_e", [P, NG, H])
            o_in = [sb(f"o_in_e{i}", [P, NG, QB]) for i in range(2)]
            r_b = [sb(f"r_b_e{i}", [P, NG, QB]) for i in range(2)]
            on = [sb(f"on_e{i}", [P, NG, QB]) for i in range(2)]
            xb = [sb(f"xb_e{i}", [P, TPB, H]) for i in range(2)]
            y = [sb(f"y_e{i}", [P, TPB, H]) for i in range(2)]
            bank = st.enter_context(nc.psum_tensor("bank_e", [P, 8, 512], F32))

            w_in = sem("w_in_e")
            in_all = [sem(f"in_all_e{i}") for i in range(2)]
            xb_in = [sem(f"xb_in_e{i}") for i in range(2)]
            on_ready = sem("on_ready_e")
            y_done = sem("y_done_e")
            y_ready = sem("y_ready_e")
            y_out = [sem(f"y_out_e{i}") for i in range(2)]
            from_start = [on_ready, y_done, y_ready] + y_out

            def blocks(eng):
                with eng.Fori(0, NB // 2) as i:
                    yield i, 0, 2 * i
                    yield i, 1, 2 * i + 1

            with nc.Block() as block:
                @block.gpsimd
                def _(pool):
                    raise_to_start(pool, from_start)

                @block.sync
                def _(sp):
                    with again(sp):
                        sp.dma_start(wp[:, :, :], Wp.rearrange("(g p) n -> p g n", p=P)).then_inc(w_in, 16)
                        for i, par, b in blocks(sp):
                            cols = ds(b * QB, QB)
                            sp.wait_ge(on_ready, START + b - 1)
                            sp.dma_start(o_in[par][:, :, :],
                                         o_dram[:, cols].rearrange("(g p) q -> p g q", p=P)).then_inc(in_all[par], 16)
                            for j in range(HG):
                                src = r_dram[:, cols].rearrange("(g j) q -> j g q", j=HG)[j:j + 1, :, :]
                                sp.dma_start(r_b[par][j * DH:(j + 1) * DH, :, :],
                                             src.broadcast_to([DH, NG, QB])).then_inc(in_all[par], 16)
                            sp.wait_ge(y_ready, START + TPB * (b - 1))
                            sp.dma_start(xb[par][:, :, :],
                                         xb_dram[cols, :].rearrange("(j p) f -> p j f", p=P)).then_inc(xb_in[par], 16)

                @block.scalar
                def _(act):
                    with again(act):
                        for i, par, b in blocks(act):
                            act.wait_ge(y_ready, START + TPB * (b + 1))
                            act.dma_start(out2[ds(b * QB, QB), :].rearrange("(j p) f -> p j f", p=P),
                                          y[par][:, :, :]).then_inc(y_out[par], 16)
                        for par in range(2):
                            act.wait_ge(y_out[par], START + 16 * NB // 2)

                @block.tensor
                def _(pe):
                    with again(pe):
                        pe.wait_ge(w_in, 16)
                        for i, par, b in blocks(pe):
                            pe.wait_ge(on_ready, START + b + 1)
                            for j in range(TPB):
                                bk = TPB * par + j
                                pe.wait_ge(y_ready, START + TPB * (b - 2) + j + 1)
                                for g in range(NG):
                                    mm = nc.tensor.matmul(bank[:, bk, :], on[par][:, g, j * P:(j + 1) * P],
                                                          wp[:, g, :], start=(g == 0), stop=(g == NG - 1))
                                mm.then_inc(y_done, 1)

                @block.vector
                def _(dve):
                    def divide(i, par, b):
                        dve.wait_ge(in_all[par], 16 * (1 + HG) * (i + 1))
                        dve.wait_ge(y_done, START + TPB * (b - 1))
                        nc.vector.tensor_tensor(on[par][:, :, :], o_in[par][:, :, :], r_b[par][:, :, :],
                                                ALU.mult).then_inc(on_ready, 1)

                    def add_residual(i, par, b):
                        dve.wait_ge(xb_in[par], 16 * (i + 1))
                        dve.wait_ge(y_out[par], START + 16 * i)
                        for j in range(TPB):
                            dve.wait_ge(y_done, START + TPB * b + j + 1)
                            nc.vector.tensor_tensor(y[par][:, j, :], bank[:, TPB * par + j, :], xb[par][:, j, :],
                                                    ALU.add).then_inc(y_ready, 1)

                    with again(dve):
                        divide(0, 0, 0)
                        with dve.Fori(0, NB // 2 - 1) as i:
                            divide(i, 1, 2 * i + 1)
                            add_residual(i, 0, 2 * i)
                            divide(i + 1, 0, 2 * i + 2)
                            add_residual(i, 1, 2 * i + 1)
                        divide(NB // 2 - 1, 1, NB - 1)
                        add_residual(NB // 2 - 1, 0, NB - 2)
                        add_residual(NB // 2 - 1, 1, NB - 1)

    with outer:
        prologue()
        attention_and_check()
        exact_epilogue()


_INS = ['x', 'ctx_1024', 'cond_1024', 'L0_xcond_Wq', 'L0_xcond_bq', 'L0_xcond_Wkv', 'L0_xcond_bkv', 'L0_xcond_Wp',
        'L0_xcond_bp', 'L0_xcond_Wss_q', 'L0_xcond_bss_q', 'L0_xcond_Wss_kv', 'L0_xcond_bss_kv']


def kernel(**inputs):
    import numpy as _np
    import concourse.bacc as _bacc
    from concourse import mybir as _mybir
    from concourse.bass_utils import run_bass_kernel_spmd as _run

    nc = _bacc.Bacc("TRN2", target_bir_lowering=False, num_devices=1)
    arrays, args = {}, []
    for name in _INS:
        a = _np.ascontiguousarray(inputs[name])
        arrays[f"in_{name}_dram"] = a
        args.append(nc.dram_tensor(f"in_{name}_dram", a.shape, _mybir.dt.from_np(a.dtype), kind="ExternalInput").ap())
    shape = tuple(inputs['x'].shape)
    args.append(nc.dram_tensor("out_dram", shape, _mybir.dt.float32, kind="ExternalOutput").ap())
    cross_attention(nc, *args)
    r = _run(nc, [arrays], core_ids=[0])
    return r.results[0]["out_dram"]
```
